# Optimizing a Trainium2 kernel written in Bass

```python
import numpy as np
import jax
import jax.numpy as jnp

def _softmax(x, axis=-1):
    return jax.nn.softmax(x, axis=axis)

def _gelu(x):
    return jax.nn.gelu(x, approximate=True)

def _silu(x):
    return jax.nn.silu(x)

def _sigmoid(x):
    return jax.nn.sigmoid(x)

def _layernorm(x, axis=-1, eps=1e-05):
    m = jnp.mean(x, axis=axis, keepdims=True)
    v = jnp.var(x, axis=axis, keepdims=True)
    return (x - m) / jnp.sqrt(v + eps)

def _scatter_add(tgt, idx, src, axis=0):
    return tgt.at[idx].add(src)

def _segment_sum(src, seg, n):
    return jax.ops.segment_sum(src, seg, n)
kernel_name = 'mk_gps_d1_gnn_r8_b07dec'

def setup_inputs(seed: int=0):
    np.random.seed(seed)
    _w = jnp.asarray

    def _rec_inputs():
        import jax
        import jax.numpy as jnp
        _gk = jax.random.key(seed)
        x = -0.0003713 + 1 * jax.random.normal(jax.random.fold_in(_gk, 1), (6250, 256), jnp.float32)
        _s = jax.random.randint(jax.random.fold_in(_gk, 2), (100000,), 0, 6250, jnp.int32)
        _d = jax.random.randint(jax.random.fold_in(_gk, 3), (100000,), 0, 6250, jnp.int32)
        _loop = jnp.arange(6250, dtype=jnp.int32)
        src = jnp.concatenate([_s, _d, _loop])
        dst = jnp.concatenate([_d, _s, _loop])
        _o = jnp.argsort(dst, stable=True)
        src = src[_o]
        dst = dst[_o]
        edge_type_8 = jax.random.randint(jax.random.fold_in(_gk, 12), (206250,), 0, 8, jnp.int32)
        return (x, src, dst, edge_type_8)
    x, src, dst, edge_type_8 = _rec_inputs()

    def _L0_gnn_setup():
        import jax, jax.numpy as jnp
        import numpy as np
        N_NODES = 6250
        N_EDGES = 37500
        N_REL = 8
        D = 256
        N_LAYERS = 3

        def _rgcn_layer(x, W, root, bias, src, dst, seg):
            agg = jax.ops.segment_sum(x[src], seg, num_segments=N_REL * N_NODES)
            agg = agg.reshape(N_REL, N_NODES, -1)
            return jnp.einsum('rnd,rde->ne', agg, W) + x @ root + bias
        key = jax.random.key(seed)
        k1, k2, k3, k4, k5 = jax.random.split(key, 5)
        x = jax.random.normal(k1, (N_NODES, D), dtype=jnp.float32)
        scale = 1.0 / np.sqrt(D)
        weights = jax.random.normal(k2, (N_LAYERS, N_REL, D, D), dtype=jnp.float32) * scale
        roots = jax.random.normal(k3, (N_LAYERS, D, D), dtype=jnp.float32) * scale
        biases = jnp.zeros((N_LAYERS, D), dtype=jnp.float32)
        edge_index = jax.random.randint(k4, (2, N_EDGES), 0, N_NODES, dtype=jnp.int64)
        edge_type = jax.random.randint(k5, (N_EDGES,), 0, N_REL, dtype=jnp.int64)
        return {'x': x, 'weights': weights, 'roots': roots, 'biases': biases, 'edge_index': edge_index, 'edge_type': edge_type}
    _L0_gnn_all = _L0_gnn_setup()
    _L0_gnn_in = {k: v for k, v in _L0_gnn_all.items() if k in ('weights', 'roots', 'biases')}
    del _L0_gnn_all

    def _L0_mix_setup():
        import jax, jax.numpy as jnp
        import numpy as np
        B, N, C = (8, 1024, 256)
        HEADS, DH, KR = (8, 32, 4)
        INNER = HEADS * DH
        FF = 4 * C
        EPS = 1e-05

        def layernorm(x, g, b):
            mu = jnp.mean(x, axis=-1, keepdims=True)
            var = jnp.mean((x - mu) ** 2, axis=-1, keepdims=True)
            return (x - mu) * jax.lax.rsqrt(var + EPS) * g + b
        key = jax.random.key(seed)
        ks = jax.random.split(key, 16)
        s = 0.02
        return {'x': jax.random.normal(ks[0], (B, N, C), jnp.float32), 'ln1_g': jnp.ones((C,), jnp.float32), 'ln1_b': jnp.zeros((C,), jnp.float32), 'Wx': jax.random.normal(ks[1], (C, INNER), jnp.float32) * s, 'bx': jnp.zeros((INNER,), jnp.float32), 'Wq': jax.random.normal(ks[2], (DH, KR), jnp.float32) * s, 'Wk': jax.random.normal(ks[3], (DH, KR), jnp.float32) * s, 'Wv': jax.random.normal(ks[4], (DH, DH), jnp.float32) * s, 'Wo': jax.random.normal(ks[5], (INNER, C), jnp.float32) * s, 'bo': jnp.zeros((C,), jnp.float32), 'ln2_g': jnp.ones((C,), jnp.float32), 'ln2_b': jnp.zeros((C,), jnp.float32), 'W1': jax.random.normal(ks[6], (C, FF), jnp.float32) * s, 'b1': jnp.zeros((FF,), jnp.float32), 'W2': jax.random.normal(ks[7], (FF, C), jnp.float32) * s, 'b2': jnp.zeros((C,), jnp.float32)}
    _L0_mix_all = _L0_mix_setup()
    _L0_mix_in = {k: v for k, v in _L0_mix_all.items() if k in ('ln1_g', 'ln1_b', 'Wx', 'bx', 'Wq', 'Wk', 'Wv', 'Wo', 'bo', 'ln2_g', 'ln2_b', 'W1', 'b1', 'W2', 'b2')}
    del _L0_mix_all

    def _L0_ffn_setup():
        import jax, jax.numpy as jnp
        import numpy as np
        NUM_EXPERTS = 8
        TOP_K = 2
        B, S, D = (8, 1024, 256)

        def _moe(tokens, router_w, w1, b1, w2, b2):
            N = tokens.shape[0]
            E = router_w.shape[0]
            logits = tokens.astype(jnp.float32) @ router_w.astype(jnp.float32).T
            probs = jax.nn.softmax(logits, axis=-1)
            rw, re = jax.lax.top_k(probs, TOP_K)
            if TOP_K > 1:
                rw = rw / jnp.maximum(rw.sum(-1, keepdims=True), 1e-12)
            rw = rw.astype(tokens.dtype)
            combine = jnp.zeros((N, E), tokens.dtype).at[jnp.arange(N)[:, None], re].set(rw)
            out = tokens
            for e in range(E):
                h = jax.nn.gelu(tokens @ w1[e] + b1[e], approximate=False)
                y = h @ w2[e] + b2[e]
                out = out + combine[:, e:e + 1] * y
            return out
        key = jax.random.key(seed)
        ks = jax.random.split(key, 4)
        scale = 1.0 / np.sqrt(D).astype(np.float32)
        return {'input_embeddings': jax.random.normal(ks[0], (B, S, D), jnp.float32), 'router_w': jax.random.normal(ks[1], (NUM_EXPERTS, D), jnp.float32) * scale, 'w1': jax.random.normal(ks[2], (NUM_EXPERTS, D, D), jnp.float32) * scale, 'b1': jnp.zeros((NUM_EXPERTS, D), jnp.float32), 'w2': jax.random.normal(ks[3], (NUM_EXPERTS, D, D), jnp.float32) * scale, 'b2': jnp.zeros((NUM_EXPERTS, D), jnp.float32)}
    _L0_ffn_all = _L0_ffn_setup()
    _L0_ffn_in = {k: v for k, v in _L0_ffn_all.items() if k in ('router_w', 'w1', 'b1', 'w2', 'b2')}
    del _L0_ffn_all
    return {'x': x, 'src': src, 'dst': dst, 'edge_type_8': edge_type_8, 'L0_gnn_weights': _L0_gnn_in['weights'], 'L0_gnn_roots': _L0_gnn_in['roots'], 'L0_gnn_biases': _L0_gnn_in['biases'], 'L0_mix_ln1_g': _L0_mix_in['ln1_g'], 'L0_mix_ln1_b': _L0_mix_in['ln1_b'], 'L0_mix_Wx': _L0_mix_in['Wx'], 'L0_mix_bx': _L0_mix_in['bx'], 'L0_mix_Wq': _L0_mix_in['Wq'], 'L0_mix_Wk': _L0_mix_in['Wk'], 'L0_mix_Wv': _L0_mix_in['Wv'], 'L0_mix_Wo': _L0_mix_in['Wo'], 'L0_mix_bo': _L0_mix_in['bo'], 'L0_mix_ln2_g': _L0_mix_in['ln2_g'], 'L0_mix_ln2_b': _L0_mix_in['ln2_b'], 'L0_mix_W1': _L0_mix_in['W1'], 'L0_mix_b1': _L0_mix_in['b1'], 'L0_mix_W2': _L0_mix_in['W2'], 'L0_mix_b2': _L0_mix_in['b2'], 'L0_ffn_router_w': _L0_ffn_in['router_w'], 'L0_ffn_w1': _L0_ffn_in['w1'], 'L0_ffn_b1': _L0_ffn_in['b1'], 'L0_ffn_w2': _L0_ffn_in['w2'], 'L0_ffn_b2': _L0_ffn_in['b2']}

def reference(x, src, dst, edge_type_8, L0_gnn_weights, L0_gnn_roots, L0_gnn_biases, L0_mix_ln1_g, L0_mix_ln1_b, L0_mix_Wx, L0_mix_bx, L0_mix_Wq, L0_mix_Wk, L0_mix_Wv, L0_mix_Wo, L0_mix_bo, L0_mix_ln2_g, L0_mix_ln2_b, L0_mix_W1, L0_mix_b1, L0_mix_W2, L0_mix_b2, L0_ffn_router_w, L0_ffn_w1, L0_ffn_b1, L0_ffn_w2, L0_ffn_b2):
    import jax
    import jax.numpy as jnp

    def _L0_gnn_ref(x, weights, roots, biases, edge_index, edge_type):
        import jax, jax.numpy as jnp
        import numpy as np
        N_NODES = 6250
        N_EDGES = 37500
        N_REL = 8
        D = 256
        N_LAYERS = 3

        def _rgcn_layer(x, W, root, bias, src, dst, seg):
            agg = jax.ops.segment_sum(x[src], seg, num_segments=N_REL * N_NODES)
            agg = agg.reshape(N_REL, N_NODES, -1)
            return jnp.einsum('rnd,rde->ne', agg, W) + x @ root + bias
        src, dst = (edge_index[0], edge_index[1])
        seg = edge_type * N_NODES + dst
        h = x
        for l in range(N_LAYERS - 1):
            h = jax.nn.relu(_rgcn_layer(h, weights[l], roots[l], biases[l], src, dst, seg))
        h = jax.nn.sigmoid(_rgcn_layer(h, weights[-1], roots[-1], biases[-1], src, dst, seg))
        return h

    def _L0_mix_ref(x, ln1_g, ln1_b, Wx, bx, Wq, Wk, Wv, Wo, bo, ln2_g, ln2_b, W1, b1, W2, b2):
        import jax, jax.numpy as jnp
        import numpy as np
        B, N, C = (8, 1024, 256)
        HEADS, DH, KR = (8, 32, 4)
        INNER = HEADS * DH
        FF = 4 * C
        EPS = 1e-05

        def layernorm(x, g, b):
            mu = jnp.mean(x, axis=-1, keepdims=True)
            var = jnp.mean((x - mu) ** 2, axis=-1, keepdims=True)
            return (x - mu) * jax.lax.rsqrt(var + EPS) * g + b
        b, n, c = x.shape
        h = layernorm(x, ln1_g, ln1_b)
        xm = h @ Wx + bx
        xm = xm.reshape(b, n, HEADS, DH).transpose(0, 2, 1, 3)
        q = jax.nn.softmax(xm @ Wq, axis=-1)
        k = jax.nn.softmax(xm @ Wk, axis=-2)
        v = xm @ Wv
        kv = jnp.einsum('bhnr,bhnd->bhrd', k, v)
        qkv = jnp.einsum('bhnr,bhrd->bhnd', q, kv)
        attn = qkv.transpose(0, 2, 1, 3).reshape(b, n, INNER) @ Wo + bo
        fx = attn + x
        h2 = layernorm(fx, ln2_g, ln2_b)
        m = jax.nn.gelu(h2 @ W1 + b1, approximate=False) @ W2 + b2
        return m + fx

    def _L0_ffn_ref(input_embeddings, router_w, w1, b1, w2, b2):
        import jax, jax.numpy as jnp
        import numpy as np
        NUM_EXPERTS = 8
        TOP_K = 2
        B, S, D = (8, 1024, 256)

        def _moe(tokens, router_w, w1, b1, w2, b2):
            N = tokens.shape[0]
            E = router_w.shape[0]
            logits = tokens.astype(jnp.float32) @ router_w.astype(jnp.float32).T
            probs = jax.nn.softmax(logits, axis=-1)
            rw, re = jax.lax.top_k(probs, TOP_K)
            if TOP_K > 1:
                rw = rw / jnp.maximum(rw.sum(-1, keepdims=True), 1e-12)
            rw = rw.astype(tokens.dtype)
            combine = jnp.zeros((N, E), tokens.dtype).at[jnp.arange(N)[:, None], re].set(rw)
            out = tokens
            for e in range(E):
                h = jax.nn.gelu(tokens @ w1[e] + b1[e], approximate=False)
                y = h @ w2[e] + b2[e]
                out = out + combine[:, e:e + 1] * y
            return out
        b, s, d = input_embeddings.shape
        tokens = input_embeddings.reshape(b * s, d)
        return _moe(tokens, router_w, w1, b1, w2, b2).reshape(b, s, d)
    edge_index = jnp.stack([src, dst])
    xn = _layernorm(x, axis=-1)
    x = x + _L0_gnn_ref(xn, L0_gnn_weights, L0_gnn_roots, L0_gnn_biases, edge_index, edge_type_8) + _L0_mix_ref(xn[None], L0_mix_ln1_g, L0_mix_ln1_b, L0_mix_Wx, L0_mix_bx, L0_mix_Wq, L0_mix_Wk, L0_mix_Wv, L0_mix_Wo, L0_mix_bo, L0_mix_ln2_g, L0_mix_ln2_b, L0_mix_W1, L0_mix_b1, L0_mix_W2, L0_mix_b2)[0]
    x = x + _L0_ffn_ref(_layernorm(x, axis=-1)[None], L0_ffn_router_w, L0_ffn_w1, L0_ffn_b1, L0_ffn_w2, L0_ffn_b2)[0]
    return x

_drawn_inputs = setup_inputs


def setup_inputs(seed=0):
    import zlib

    import numpy as np

    out = dict(_drawn_inputs(seed))
    spreads = {'L0_gnn_biases': (0.0, 0.763),
     'L0_mix_ln1_g': (1.0, 0.6),
     'L0_mix_ln1_b': (0.0, 0.8),
     'L0_mix_bx': (0.0, 0.8),
     'L0_mix_bo': (0.0, 0.567),
     'L0_mix_ln2_g': (1.0, 0.6),
     'L0_mix_ln2_b': (0.0, 2.0),
     'L0_mix_b1': (0.0, 1.262),
     'L0_mix_b2': (0.0, 0.527),
     'L0_ffn_b1': (0.0, 0.499),
     'L0_ffn_b2': (0.0, 0.335)}
    factors = {'L0_mix_Wx': 8.0, 'L0_mix_Wq': 8.0, 'L0_mix_Wk': 8.0, 'L0_mix_Wv': 8.0, 'L0_mix_Wo': 8.0}
    for name, (base, spread) in spreads.items():
        noise = np.random.default_rng([zlib.crc32(name.encode()), seed]).standard_normal(out[name].shape)
        drawn = base * np.exp(spread * noise) if base else spread * noise
        out[name] = jnp.asarray(drawn.astype(out[name].dtype))
    for name, factor in factors.items():
        out[name] = (out[name] * factor).astype(out[name].dtype)
    return out
```

```python
import numpy as np
import concourse.bass as bass
from concourse import mybir
from concourse.alu_op_type import AluOpType as ALU
from contextlib import ExitStack

FP32 = mybir.dt.float32
I32 = mybir.dt.int32
U32 = mybir.dt.uint32
ACT = mybir.ActivationFunctionType
AX = mybir.AxisListType
EPS = 1e-5

WIN = 125
WIN_A = 112
TILE = 128
TILES = 2
RING = 13
GROUP_A = 7


def gps_program(nc, t):
    nodes, D = t["x"].shape
    edges = t["src"].shape[0]
    R = t["L0_gnn_weights"].shape[1]
    ROWS = R + 1
    K = D // 128
    NW = nodes // WIN
    assert nodes % WIN == 0 and NW % 2 == 0
    body_edges = TILE * TILES * RING
    BODIES = -(-edges // body_edges)
    CHUNKS = BODIES * RING
    NT = CHUNKS * TILES
    TB = -(-NT // 128)
    full_tiles = edges // TILE
    rest = edges - full_tiles * TILE
    full_blocks = full_tiles // 128
    last_rows = full_tiles - full_blocks * 128
    H, DH = 8, 32
    KR = t["L0_mix_Wq"].shape[1]
    HK = H * KR
    FF = t["L0_mix_W1"].shape[1]
    FJ = FF // 128
    E = t["L0_ffn_w1"].shape[0]
    PADDED = 1 << 20
    QK = 4 * KR
    BDW = 2 * QK + 128

    table = [nc.dram_tensor(f"table{l}", [nodes * ROWS, D], FP32).ap() for l in range(3)]
    table_nodes = [a.rearrange("(n r) d -> n (r d)", r=ROWS) for a in table]
    xn_dram = nc.dram_tensor("xn_scratch", [nodes, D], FP32).ap()
    res_dram = nc.dram_tensor("res_scratch", [nodes, D], FP32).ap()
    tile_ends_dram = nc.dram_tensor("tile_ends", [2, TB * 128], FP32).ap()

    with ExitStack() as ctx:
        ctx.enter_context(nc.allow_non_contiguous_dma(reason="a few vectors go to a feature a partition"))

        def sb(name, shape, dt=FP32):
            return ctx.enter_context(nc.sbuf_tensor(name, shape, dt))

        def sem(name):
            return ctx.enter_context(nc.semaphore(name))

        ident = sb("ident", [128, 128])
        iota_win = sb("iota_win", [128, WIN])
        win_base = sb("win_base", [128, NW])
        neg_half = sb("neg_half", [WIN, 1])
        eps_col = sb("eps_col", [WIN, 1])
        zero_col = sb("zero_col", [128, 1])
        ones_row = sb("ones_row", [HK, WIN])
        head_mask = sb("head_mask", [HK, D])
        iota_e = sb("iota_e", [WIN, E])
        gather_idx = sb("gather_idx", [128, TB * 128], I32)
        targets = sb("targets", [128, TB * 128])
        idx_now = sb("idx_now", [128, RING * TILES], U32)
        ring = sb("ring", [128, RING * TILES * D])
        onehot = [sb(f"onehot{i}", [128, WIN]) for i in range(TILES)]
        W = sb("W", [128, K, ROWS * D])
        bias_bc = sb("bias_bc", [WIN, 3, D])
        y_stage = [sb(f"y_stage{i}", [WIN, ROWS * D]) for i in range(2)]
        x_in = [sb(f"x_in{i}", [WIN, D]) for i in range(2)]
        xn_in = [sb(f"xn_in{i}", [WIN, D]) for i in range(2)]
        base_in = [sb(f"base_in{i}", [WIN, D]) for i in range(2)]
        hT = sb("hT", [128, K, WIN])
        h_win = sb("h_win", [WIN, D])
        xhat = sb("xhat", [WIN, D])
        xhatT = sb("xhatT", [128, K, WIN])
        xmT = sb("xmT", [128, K, WIN])
        stats = sb("stats", [WIN, 6])
        mv = sb("mv", [WIN, 2])
        rstd = sb("rstd", [WIN, 1])
        ln1_scale = sb("ln1_scale", [WIN, NW])
        ln1_shift = sb("ln1_shift", [WIN, NW])
        Wx = sb("Wx", [128, K, D])
        Wo = sb("Wo", [128, K, D])
        Wqkv = sb("Wqkv", [128, BDW])
        W1 = sb("W1", [128, K, FF])
        W2 = sb("W2", [128, FJ, D])
        cols = sb("cols", [128, 5, K])
        b1_col = sb("b1_col", [128, FJ])
        mix_bc = sb("mix_bc", [WIN, 2, D])
        qk_all = sb("qk_all", [WIN, NW * K, 2 * QK])
        kexp = sb("kexp", [WIN, NW, HK])
        qk_max = sb("qk_max", [WIN, NW * K, 4])
        qk_sum = sb("qk_sum", [WIN, NW * K, 4])
        VW = D + 1
        big_cols = max(NW * VW, 4 * E * D)
        big = sb("big", [128, big_cols])
        v_all = big[0:WIN, 0:NW * VW].rearrange("p (w d) -> p w d", d=VW)
        w1e = big[:, 0:K * E * D].rearrange("p (e k d) -> p e k d", e=E, k=K)
        w2e = big[:, K * E * D:2 * K * E * D].rearrange("p (e k d) -> p e k d", e=E, k=K)
        b1e = sb("b1e", [128, E, K])
        b2e = sb("b2e", [E, D])
        rwT = sb("rwT", [128, K, E])
        kmax_part = sb("kmax_part", [WIN, HK])
        kmax = sb("kmax", [HK, 1])
        kdiag = sb("kdiag", [HK, HK])
        kv_recip = sb("kv_recip", [HK, 1])
        kv_scaled = sb("kv_scaled", [HK, D])
        kv = sb("kv", [HK, D])
        kvT = sb("kvT", [128, K, HK])
        kvWo = sb("kvWo", [HK, D])
        q_cur = sb("q_cur", [WIN, HK])
        qT = sb("qT", [HK, WIN])
        fx = sb("fx", [WIN, D])
        r0 = sb("r0", [WIN, D])
        gT = sb("gT", [128, FJ, WIN])
        res_win = sb("res_win", [WIN, D])
        small = sb("small", [WIN, 16])
        top8 = sb("top8", [WIN, 8])
        top8_idx = sb("top8_idx", [WIN, 8], U32)
        top_idx = sb("top_idx", [WIN, 2])
        probs = sb("probs", [WIN, E])
        pick = sb("pick", [WIN, 2, E])
        combine = sb("combine", [WIN, E])
        combT = sb("combT", [E, WIN])
        acc = sb("acc", [WIN, D])
        out_win = [sb(f"out_win{i}", [WIN, D]) for i in range(2)]
        NB_INTS = NW + 3
        bounds = sb("bounds", [1, NB_INTS], I32)
        bounds_f = sb("bounds_f", [NW, 8])
        bounds_row = sb("bounds_row", [1, 5, NB_INTS])

        PREP = TB * 128
        prep_i = big[:, 0:PREP].bitcast(I32)
        prep_f = big[:, PREP:2 * PREP]
        prep_d = big[:, 2 * PREP:3 * PREP].bitcast(I32)
        prep_df = big[:, 3 * PREP:4 * PREP]
        prep_t = big[:, 4 * PREP:5 * PREP].bitcast(I32)
        assert 5 * PREP <= big_cols
        SP_ = max(n for n in range(1, 129) if edges % n == 0)
        ordC = edges // SP_
        assert 3 * ordC <= RING * TILES * D
        order_a = ring[:, 0:ordC].bitcast(I32)
        order_b = ring[:, ordC:2 * ordC].bitcast(I32)
        order_c = ring[:, 2 * ordC:3 * ordC]
        order_cnt = sb("order_cnt", [128, 1])
        ones_col = sb("ones_col", [128, 1])
        ends_bc = big[0:NW, 5 * PREP:5 * PREP + 2 * NT].rearrange("p (i t) -> p i t", i=2)
        ends_cmp = big[0:NW, 5 * PREP + 2 * NT:5 * PREP + 2 * NT + CHUNKS]
        assert 5 * PREP + 2 * NT + CHUNKS <= big_cols
        ends_row = sb("ends_row", [128, 2, TB])
        thresholds = sb("thresholds", [NW, 1])

        def ps(name, shape):
            return ctx.enter_context(nc.psum_tensor(name, shape, FP32))
        ps_out = ps("ps_out", [128, 512])
        ps_tr = ps("ps_tr", [128, 512])
        ps_y = [ps(f"ps_y{i}", [128, 512]) for i in range(3)]
        ps_a = ps("ps_a", [128, 512])
        ps_b = ps("ps_b", [128, 512])
        ps_c = ps("ps_c", [128, 512])

        waits_apart = sem("waits_apart")
        consts_made = sem("consts_made")
        prep_zeroed = sem("prep_zeroed")
        edges_loaded = sem("edges_loaded")
        prep_chain = sem("prep_chain")
        prep_ready = sem("prep_ready")
        prep_tr = sem("prep_tr")
        prep_ev = sem("prep_ev")
        ends_stored = sem("ends_stored")
        ends_loaded = sem("ends_loaded")
        bounds_tr = sem("bounds_tr")
        bounds_done = sem("bounds_done")
        W_loaded = sem("W_loaded")
        gnn_bias_loaded = sem("gnn_bias_loaded")
        mix_loaded = sem("mix_loaded")
        moe_loaded = sem("moe_loaded")
        x_loaded = [sem(f"x_loaded{i}") for i in range(2)]
        xn_loaded = [sem(f"xn_loaded{i}") for i in range(2)]
        base_loaded = [sem(f"base_loaded{i}") for i in range(2)]
        var_ready = sem("var_ready")
        rstd_ready = sem("rstd_ready")
        dve_chain = sem("dve_chain")
        xn_ready = sem("xn_ready")
        ln1_ready = sem("ln1_ready")
        xn_stored = [sem(f"xn_stored{i}") for i in range(2)]
        tr_done = sem("tr_done")
        hT_ready = sem("hT_ready")
        y_done = sem("y_done")
        y_evac_act = sem("y_evac_act")
        y_evac_dve = sem("y_evac_dve")
        table_stored = [sem(f"table_stored{i}") for i in range(2)]
        idx_loaded = [sem("idx_loaded_a"), sem("idx_loaded_b")]
        gathered = [sem(f"gathered{s}") for s in range(RING)]
        chunks_ready = sem("chunks_ready")
        slots_free = sem("slots_free")
        onehot_ready = sem("onehot_ready")
        onehot_used = sem("onehot_used")
        out_done = sem("out_done")
        h_ready = sem("h_ready")
        xhat_ready = sem("xhat_ready")
        mixT_done = sem("mixT_done")
        xhatT_ready = sem("xhatT_ready")
        xm_done = sem("xm_done")
        xmT_ready = sem("xmT_ready")
        qkv_done = sem("qkv_done")
        qk_copied = sem("qk_copied")
        v_copied = sem("v_copied")
        mid_dve = sem("mid_dve")
        mid_ops = sem("mid_ops")
        mid_act = sem("mid_act")
        mid_pe = sem("mid_pe")
        q_ready = sem("q_ready")
        qT_done = sem("qT_done")
        qT_ready = sem("qT_ready")
        attn_done = sem("attn_done")
        std_ready = sem("std_ready")
        ff_done = sem("ff_done")
        gelu_done = sem("gelu_done")
        ffo_done = sem("ffo_done")
        res_ready = sem("res_ready")
        res_stored = sem("res_stored")
        tanh_ready = sem("tanh_ready")
        t_ready = sem("t_ready")
        logits_done = sem("logits_done")
        lmax_ready = sem("lmax_ready")
        rexp_ready = sem("rexp_ready")
        comb_ready = sem("comb_ready")
        combT_done = sem("combT_done")
        combT_ready = sem("combT_ready")
        b2_done = sem("b2_done")
        up_done = sem("up_done")
        act_done = sem("act_done")
        down_done = sem("down_done")
        acc_done = sem("acc_done")
        out_stored = [sem(f"out_stored{i}") for i in range(2)]

        class Chain:
            def __init__(self, s, eng):
                self.s, self.eng, self.n = s, eng, 0

            def __call__(self, ins, base=0):
                self.n += 1
                ins.then_inc(self.s, 1)
                self.eng.wait_ge(self.s, base + self.n)

        EDGE_DMAS = (3 if full_blocks else 2) * 3 + 3
        N_MIX = 4 + 5 * K + FJ + 2 + 4 * 3 + 2 * E + 1

        def apart(eng):
            eng.sem_inc(waits_apart, 1)

        def stored_before(phase, half):
            return half * 32 + phase * 32 * (NW // 2)

        S_CHAIN = 4
        P2_CHAIN = 6
        P3_CHAIN = 15

        block = ctx.enter_context(nc.Block())

        def read_int(eng, at, top):
            ap = bounds[0:1, bass.ds(at, 1)] if not isinstance(at, int) else bounds[0:1, at:at + 1]
            return eng.value_load(ap, min_val=0, max_val=top)

        LAST_TOP = (CHUNKS - 1) * NW

        def windows(eng, body):
            with eng.Fori(0, NW // 2) as half:
                for parity in range(2):
                    body(half * 2 + parity, parity, half)

        @block.sync
        def _(sp):
            sp.wait_ge(prep_zeroed, 1)
            for name, dst in (("src", prep_i), ("edge_type_8", prep_t), ("dst", prep_d)):
                a = t[name]
                v = dst[:, 0:TB * 128].rearrange("p (b f) -> p b f", f=128)
                if full_blocks:
                    sp.dma_start(v[:, 0:full_blocks, :], a[0:full_blocks * 128 * TILE]
                                 .rearrange("(b p f) -> p b f", p=128, f=TILE)).then_inc(edges_loaded, 16)
                sp.dma_start(v[0:last_rows, full_blocks, :],
                             a[full_blocks * 128 * TILE:full_tiles * TILE]
                             .rearrange("(p f) -> p f", f=TILE)).then_inc(edges_loaded, 16)
                sp.dma_start(v[last_rows:last_rows + 1, full_blocks, 0:rest],
                             a[full_tiles * TILE:edges].rearrange("(p f) -> p f", p=1)).then_inc(edges_loaded, 16)
            a = t["dst"]
            sp.dma_start(order_a[0:SP_, :], a.rearrange("(p f) -> p f", p=SP_)).then_inc(edges_loaded, 16)
            sp.dma_start(order_b[0:SP_ - 1, :], a[1:1 + (SP_ - 1) * ordC]
                         .rearrange("(p f) -> p f", p=SP_ - 1)).then_inc(edges_loaded, 16)
            sp.dma_start(order_b[SP_ - 1:SP_, 0:ordC - 1], a[1 + (SP_ - 1) * ordC:edges]
                         .rearrange("(p f) -> p f", p=1)).then_inc(edges_loaded, 16)
            sp.wait_ge(ends_stored, 1)
            for i in range(2):
                sp.dma_start(tile_ends_dram[i, :].rearrange("(b p) -> p b", p=128),
                             ends_row[:, i, :]).then_inc(ends_stored, 16)
            sp.wait_ge(ends_stored, 1 + 32)
            sp.dma_start(ends_bc[:, :, :], tile_ends_dram[:, 0:NT].unsqueeze(0)
                         .broadcast_to([NW, 2, NT])).then_inc(ends_loaded, 16)

            sp.wait_ge(prep_ev, 2 * TB)
            groups = ((0, GROUP_A), (GROUP_A, RING))
            for g, (s0, s1) in enumerate(groups):
                sp.dma_start(idx_now[:, s0 * TILES:s1 * TILES],
                             gather_idx[:, s0 * TILES:s1 * TILES].bitcast(U32)).then_inc(idx_loaded[g], 16)
            sp.wait_ge(bounds_done, 1)
            passes = read_int(sp, NW, NW)
            turns = sp.snap(passes * (BODIES * 3))
            with sp.Fori(0, turns) as turn:
                nxt = sp.snap(((turn + 1) % BODIES) * (RING * TILES))
                for g, (s0, s1) in enumerate(groups):
                    for s in range(s0, s1):
                        sp.wait_ge(gathered[s], (turn + 1) * (16 * TILES))
                        sp.sem_inc(chunks_ready, 1)
                    sp.dma_start(idx_now[:, s0 * TILES:s1 * TILES],
                                 gather_idx[:, bass.ds(nxt + s0 * TILES, (s1 - s0) * TILES)]
                                 .bitcast(U32)).then_inc(idx_loaded[g], 16)
            sp.wait_ge(idx_loaded[0], turns * 16 + 16)
            sp.wait_ge(idx_loaded[1], turns * 16 + 16)
            apart(sp)

        @block.gpsimd
        def _(pool):
            lo = full_blocks * 128
            nc.gpsimd.memset(prep_i[:, lo:TB * 128], 0)
            nc.gpsimd.memset(prep_t[:, lo:TB * 128], 0)
            nc.gpsimd.memset(order_b[:, ordC - 1:ordC], PADDED)
            nc.gpsimd.memset(prep_d[:, lo:TB * 128], PADDED).then_inc(prep_zeroed, 1)
            nc.gpsimd.memset(ident[:], 1.0).then_inc(consts_made, 1)
            pool.wait_ge(consts_made, 1)
            nc.gpsimd.affine_select(out=ident[:], in_=ident[:], compare_op=ALU.is_equal, fill=0.0,
                                    base=0, pattern=[[-1, 128]], channel_multiplier=1).then_inc(consts_made, 1)
            nc.gpsimd.iota(iota_win[:, :], pattern=[[1, WIN]], base=0, channel_multiplier=0,
                           allow_small_or_imprecise_dtypes=True)
            nc.gpsimd.iota(win_base[:, :], pattern=[[WIN, NW]], base=0, channel_multiplier=0,
                           allow_small_or_imprecise_dtypes=True)
            nc.gpsimd.iota(iota_e[:, :], pattern=[[1, E]], base=0, channel_multiplier=0,
                           allow_small_or_imprecise_dtypes=True)
            nc.gpsimd.iota(thresholds[:, :], pattern=[[0, 1]], base=WIN, channel_multiplier=WIN,
                           allow_small_or_imprecise_dtypes=True)
            nc.gpsimd.memset(neg_half[:], -0.5)
            nc.gpsimd.memset(eps_col[:], EPS)
            nc.gpsimd.memset(zero_col[:], 0.0)
            nc.gpsimd.memset(ones_row[:], 1.0)
            nc.gpsimd.memset(ones_col[:], 1.0)
            nc.gpsimd.memset(Wqkv[:], 0.0)
            nc.gpsimd.memset(head_mask[:], 1.0).then_inc(consts_made, 1)
            pool.wait_ge(consts_made, 3)
            mask = head_mask[:, :].rearrange("p (h d) -> p h d", h=H)
            nc.gpsimd.affine_select(out=mask, in_=mask, compare_op=ALU.is_ge, fill=0.0,
                                    base=0, pattern=[[-KR, H], [0, DH]], channel_multiplier=1).then_inc(consts_made, 1)
            pool.wait_ge(consts_made, 4)
            nc.gpsimd.affine_select(out=mask, in_=mask, compare_op=ALU.is_ge, fill=0.0,
                                    base=KR - 1, pattern=[[KR, H], [0, DH]], channel_multiplier=-1).then_inc(consts_made, 1)
            pool.wait_ge(consts_made, 5)
            with pool.Fori(0, 2 * NW) as i:
                pool.wait_ge(var_ready, i + 1)
                nc.gpsimd.tensor_tensor(rstd[:, :], mv[:, 1:2], neg_half[:, :], ALU.pow).then_inc(rstd_ready, 1)

            pool.wait_ge(bounds_done, 1)
            passes = read_int(pool, NW, NW)
            layer_turns = pool.snap(passes * BODIES)
            for l in range(3):
                for i in range(2):
                    pool.wait_ge(table_stored[i], 32 * (NW // 2) * (l + 1))
                with pool.Fori(0, layer_turns) as i:
                    turn = pool.snap(layer_turns * l + i)
                    for s in range(RING):
                        if s in (0, GROUP_A):
                            pool.wait_ge(idx_loaded[int(s == GROUP_A)], turn * 16 + 16)
                        pool.wait_ge(slots_free, turn * RING + (s + 1))
                        apart(pool)
                        for j in range(TILES):
                            c = s * TILES + j
                            nc.gpsimd.indirect_dma_start(
                                ring[:, c * D:(c + 1) * D], None, table[l],
                                bass.IndirectOffsetOnAxis(ap=idx_now[:, c:c + 1], axis=0)).then_inc(gathered[s], 16)

        @block.scalar
        def _(act):
            def evac_y(phase, w, parity, half):
                T = w + phase * NW
                """Banks 0, 2 and 3 of a transform: the table rows of relations 0-1, 4-5, 6-7."""
                act.wait_ge(table_stored[parity], stored_before(phase, half))
                for n, b in enumerate((0, 2, 3)):
                    act.wait_ge(y_done, T * 5 + (b + 1))
                    nc.scalar.copy(y_stage[parity][:, b * 2 * D:(b + 1) * 2 * D],
                                   ps_y[b % 3][0:WIN, 0:2 * D]).then_inc(y_evac_act, 1)

            def store_y(T, w, parity, l):
                act.wait_ge(y_evac_act, T * 3 + 3)
                act.wait_ge(y_evac_dve, T * 2 + 2)
                for p0, p1 in ((0, WIN_A), (WIN_A, WIN)):
                    act.dma_start(table_nodes[l][bass.ds(w * WIN + p0, p1 - p0), :],
                                  y_stage[parity][p0:p1, :]).then_inc(table_stored[parity], 16)

            def copy_hT(T, products=None):
                act.wait_ge(y_done, T * 5 if products is None else products)
                act.wait_ge(tr_done, T + 1)
                nc.scalar.copy(hT[:, :, :], ps_tr[:, 0:K * WIN].rearrange("p (k n) -> p k n", k=K)
                               ).then_inc(hT_ready, 1)

            def rows(a, w):
                return a[bass.ds(w * WIN, WIN), :]

            def load_W(l):
                for k in range(K):
                    act.dma_start(W[:, k, 0:R * D].rearrange("p (r e) -> p r e", r=R),
                                  t["L0_gnn_weights"][l, :, k * 128:(k + 1) * 128, :]
                                  .rearrange("r p e -> p r e")).then_inc(W_loaded, 16)
                act.dma_start(W[:, :, R * D:ROWS * D],
                              t["L0_gnn_roots"][l].rearrange("(k p) e -> p k e", p=128)).then_inc(W_loaded, 16)

            for parity in range(2):
                act.dma_start(x_in[parity][:, :], t["x"][parity * WIN:(parity + 1) * WIN, :]
                              ).then_inc(x_loaded[parity], 16)
            load_W(0)
            for l in range(3):
                act.dma_start(bias_bc[:, l, :], t["L0_gnn_biases"][l:l + 1, :].broadcast_to([WIN, D])
                              ).then_inc(gnn_bias_loaded, 16)
            act.wait_ge(consts_made, 5)
            n_mix = 0

            def mix(dst, src):
                nonlocal n_mix
                n_mix += 1
                act.dma_start(dst, src).then_inc(mix_loaded, 16)
            mix(Wx[:, :, :], t["L0_mix_Wx"].rearrange("(k p) e -> p k e", p=128))
            mix(Wo[:, :, :], t["L0_mix_Wo"].rearrange("(k p) e -> p k e", p=128))
            mix(W1[:, :, :], t["L0_mix_W1"].rearrange("(k p) e -> p k e", p=128))
            mix(W2[:, :, :], t["L0_mix_W2"].rearrange("(j p) e -> p j e", p=128))
            for i, name in enumerate(("ln1_g", "ln1_b", "bx", "ln2_g", "ln2_b")):
                for k in range(K):
                    mix(cols[:, i, k:k + 1], t["L0_mix_" + name][k * 128:(k + 1) * 128].unsqueeze(1))
            for j in range(FJ):
                mix(b1_col[:, j:j + 1], t["L0_mix_b1"][j * 128:(j + 1) * 128].unsqueeze(1))
            mix(mix_bc[:, 0, :], t["L0_mix_bo"].unsqueeze(0).broadcast_to([WIN, D]))
            mix(mix_bc[:, 1, :], t["L0_mix_b2"].unsqueeze(0).broadcast_to([WIN, D]))
            for j in range(4):
                mix(Wqkv[j * DH:(j + 1) * DH, j * KR:(j + 1) * KR], t["L0_mix_Wq"])
                mix(Wqkv[j * DH:(j + 1) * DH, QK + j * KR:QK + (j + 1) * KR], t["L0_mix_Wk"])
                mix(Wqkv[j * DH:(j + 1) * DH, 2 * QK + j * DH:2 * QK + (j + 1) * DH], t["L0_mix_Wv"])
            for e in range(E):
                mix(rwT[:, :, e:e + 1], t["L0_ffn_router_w"][e, :].rearrange("(k p) -> p k", p=128).unsqueeze(2))
                mix(b1e[:, e, :].unsqueeze(2), t["L0_ffn_b1"][e, :].rearrange("(k p) -> p k", p=128).unsqueeze(2))
            mix(b2e[:, :], t["L0_ffn_b2"])
            assert n_mix == N_MIX

            def phase0(w, parity, half, last):
                act.wait_ge(xn_ready, w + 1)
                act.dma_start(rows(xn_dram, w), xn_in[parity][:, :]).then_inc(xn_stored[parity], 16)
                if not last:
                    act.dma_start(x_in[parity][:, :], rows(t["x"], w + 2)).then_inc(x_loaded[parity], 16)
                copy_hT(w)
                evac_y(0, w, parity, half)
                store_y(w, w, parity, 0)
            with act.Fori(0, NW // 2 - 1) as half:
                for parity in range(2):
                    phase0(half * 2 + parity, parity, half, False)
            for parity in range(2):
                phase0(NW - 2 + parity, parity, NW // 2 - 1, True)

            act.wait_ge(y_done, 5 * NW)
            load_W(1)
            for i in range(2):
                act.wait_ge(table_stored[i], 32 * (NW // 2))
                act.wait_ge(xn_stored[i], 16 * (NW // 2))
            act.wait_ge(mix_loaded, 16 * n_mix)

            def base_rows(l, w):
                return table_nodes[l][bass.ds(w * WIN, WIN), R * D:ROWS * D]

            def load_base(l, w, parity):
                act.dma_start(base_in[parity][:, :], base_rows(l, w)).then_inc(base_loaded[parity], 16)

            def phase1(w, parity, half):
                load_base(0, w, parity)
                act.dma_start(xn_in[parity][:, :], rows(xn_dram, w)).then_inc(xn_loaded[parity], 16)
                act.wait_ge(xn_loaded[parity], half * 16 + 16)
                act.wait_ge(ln1_ready, NW)
                nc.scalar.activation(xhat[:, :], xn_in[parity][:, :], ACT.Identity,
                                     scale=ln1_scale[:, bass.ds(w, 1)],
                                     bias=ln1_shift[:, bass.ds(w, 1)]).then_inc(xhat_ready, 1)
                act.wait_ge(out_done, w + 1)
                nc.scalar.activation(h_win[:, :], ps_out[0:WIN, 0:D], ACT.Relu).then_inc(h_ready, 1)
                act.wait_ge(mixT_done, w + 1)
                for k in range(K):
                    last = nc.scalar.activation(xhatT[:, k, :], ps_a[:, k * WIN:(k + 1) * WIN], ACT.Identity,
                                                scale=cols[:, 0, k:k + 1], bias=cols[:, 1, k:k + 1])
                last.then_inc(xhatT_ready, 1)
                copy_hT(NW + w)
                act.wait_ge(xm_done, w + 1)
                for k in range(K):
                    last = nc.scalar.activation(xmT[:, k, :], ps_b[:, k * WIN:(k + 1) * WIN], ACT.Identity,
                                                scale=1.0, bias=cols[:, 2, k:k + 1])
                last.then_inc(xmT_ready, 1)
                evac_y(1, w, parity, half)
                act.wait_ge(qkv_done, w + 1)
                nc.scalar.copy(v_all[:, bass.ds(w, 1), 0:D].rearrange("p w (c d) -> p (w c) d", c=K),
                               ps_c[0:WIN, 0:K * BDW].rearrange("p (c d) -> p c d", c=K)[:, :, 2 * QK:BDW]
                               ).then_inc(v_copied, 1)
                store_y(NW + w, w, parity, 1)
            act.wait_ge(bounds_done, 1)
            windows(act, phase1)

            act.wait_ge(mid_dve, 1)
            nc.scalar.activation(qk_all[:, :, 0:QK], qk_all[:, :, 0:QK], ACT.Exp).then_inc(mid_act, 1)
            act.wait_ge(mid_dve, 2)
            nc.scalar.activation(kexp[:, :, :], kexp[:, :, :], ACT.Exp).then_inc(mid_act, 1)
            act.wait_ge(y_done, 5 * 2 * NW)
            load_W(2)
            for i in range(2):
                act.wait_ge(table_stored[i], 2 * 32 * (NW // 2))
            act.wait_ge(mid_dve, 3)

            XN0 = 16 * (NW // 2)

            def phase2(w, parity, half):
                nc.scalar.copy(q_cur[:, :].rearrange("p (c j) -> p c j", c=K),
                               qk_all[:, bass.ds(w * K, K), 0:QK]).then_inc(q_ready, 1)
                load_base(1, w, parity)
                act.dma_start(xn_in[parity][:, :], rows(xn_dram, w)).then_inc(xn_loaded[parity], 16)
                act.dma_start(x_in[parity][:, :], rows(t["x"], w)).then_inc(x_loaded[parity], 16)
                act.wait_ge(qT_done, w + 1)
                nc.scalar.copy(qT[:, :], ps_a[0:HK, 0:WIN]).then_inc(qT_ready, 1)
                act.wait_ge(out_done, NW + w + 1)
                nc.scalar.activation(h_win[:, :], ps_out[0:WIN, 0:D], ACT.Relu).then_inc(h_ready, 1)
                copy_hT(2 * NW + w)
                act.wait_ge(var_ready, 2 * NW + w + 1)
                nc.scalar.activation(rstd[:, :], mv[:, 1:2], ACT.Sqrt, bias=eps_col[:, :]).then_inc(std_ready, 1)
                evac_y(2, w, parity, half)
                act.wait_ge(mixT_done, NW + w + 1)
                for k in range(K):
                    last = nc.scalar.activation(xhatT[:, k, :], ps_a[:, k * WIN:(k + 1) * WIN], ACT.Identity,
                                                scale=cols[:, 3, k:k + 1], bias=cols[:, 4, k:k + 1])
                last.then_inc(xhatT_ready, 1)
                for j in range(FJ):
                    if j % 4 == 0:
                        act.wait_ge(ff_done, w * 2 + (j // 4 + 1))
                    bank = (ps_b, ps_c)[j // 4]
                    nc.scalar.activation(gT[:, j, :], bank[:, (j % 4) * WIN:(j % 4 + 1) * WIN], ACT.Gelu,
                                         bias=b1_col[:, j:j + 1]).then_inc(gelu_done, 1)
                store_y(2 * NW + w, w, parity, 2)
                act.wait_ge(res_ready, w + 1)
                act.dma_start(rows(res_dram, w), res_win[:, :]).then_inc(res_stored, 16)
            windows(act, phase2)

            act.wait_ge(mid_pe, 5)
            for e in range(E):
                act.dma_start(w1e[:, e, :, :], t["L0_ffn_w1"][e].rearrange("(k p) f -> p k f", p=128)).then_inc(moe_loaded, 16)
                act.dma_start(w2e[:, e, :, :], t["L0_ffn_w2"][e].rearrange("(k p) f -> p k f", p=128)).then_inc(moe_loaded, 16)
            for i in range(2):
                act.wait_ge(table_stored[i], 3 * 32 * (NW // 2))
            act.wait_ge(res_stored, 16 * NW)

            def phase3(w, parity, half):
                load_base(2, w, parity)
                act.dma_start(xn_in[parity][:, :], rows(res_dram, w)).then_inc(xn_loaded[parity], 16)
                act.wait_ge(out_done, 2 * NW + w + 1)
                nc.scalar.activation(h_win[:, :], ps_out[0:WIN, 0:D], ACT.Tanh, scale=0.5).then_inc(tanh_ready, 1)
                act.wait_ge(var_ready, 3 * NW + w + 1)
                nc.scalar.activation(rstd[:, :], mv[:, 1:2], ACT.Sqrt, bias=eps_col[:, :]).then_inc(std_ready, 1)
                copy_hT(3 * NW + w, 3 * NW * 5)
                act.wait_ge(lmax_ready, w + 1)
                nc.scalar.activation(probs[:, :], ps_a[0:WIN, 0:E], ACT.Exp, bias=small[:, 0:1],
                                     accum_out=small[:, 1:2]).then_inc(rexp_ready, 1)
                for e in range(E):
                    act.wait_ge(up_done, w * E + (e + 1))
                    if e >= 2:
                        act.wait_ge(down_done, w * E + (e - 1))
                    for f in range(K):
                        last = nc.scalar.activation(gT[:, (e % 2) * K + f, :], ps_y[e % 2][:, f * WIN:(f + 1) * WIN],
                                                    ACT.Gelu, bias=b1e[:, e, f:f + 1])
                    last.then_inc(act_done, 1)
                    if e == 0:
                        act.wait_ge(combT_done, w + 1)
                        nc.scalar.copy(combT[:, :], ps_a[0:E, 256:256 + WIN]).then_inc(combT_ready, 1)
                act.wait_ge(acc_done, w * E + E)
                act.dma_start(rows(t["out"], w), out_win[parity][:, :]).then_inc(out_stored[parity], 16)
            windows(act, phase3)
            for i in range(2):
                act.wait_ge(out_stored[i], 16 * (NW // 2))

        @block.vector
        def _(dve):
            def evac_y(phase, w, parity, half):
                T = w + phase * NW
                """Bank 1 (relations 2-3) and bank 4 (the root's product, with the bias)."""
                dve.wait_ge(table_stored[parity], stored_before(phase, half))
                dve.wait_ge(y_done, T * 5 + 2)
                nc.vector.tensor_copy(y_stage[parity][:, 2 * D:4 * D], ps_y[1][0:WIN, 0:2 * D]).then_inc(y_evac_dve, 1)
                dve.wait_ge(y_done, T * 5 + 5)
                nc.vector.tensor_tensor(y_stage[parity][:, R * D:ROWS * D], ps_y[1][0:WIN, 0:D],
                                        bias_bc[:, phase, :], ALU.add).then_inc(y_evac_dve, 1)

            once = Chain(prep_chain, dve)
            dve.wait_ge(edges_loaded, 16 * EDGE_DMAS)
            dve.wait_ge(consts_made, 5)
            nc.vector.scalar_tensor_tensor(out=prep_f, in0=prep_i, scalar=float(ROWS), in1=prep_t,
                                           op0=ALU.mult, op1=ALU.add)
            nc.vector.tensor_copy(prep_df, prep_d).then_inc(prep_ready, 1)
            d3 = prep_d.rearrange("p (b f) -> p b f", f=128)
            nc.vector.tensor_reduce(ends_row[:, 0, :], d3, axis=AX.X, op=ALU.min)
            nc.vector.tensor_reduce(ends_row[:, 1, :], d3, axis=AX.X, op=ALU.max).then_inc(ends_stored, 1)
            once(nc.vector.memset(order_cnt[:], 0.0))
            once(nc.vector.tensor_tensor(order_c[0:SP_, :], order_a[0:SP_, :], order_b[0:SP_, :], ALU.is_gt))
            once(nc.vector.tensor_reduce(order_cnt[0:SP_, :], order_c[0:SP_, :], axis=AX.X, op=ALU.add))
            for i in range(2 * TB):
                b = i // 2
                dve.wait_ge(prep_tr, i + 1)
                dst = (gather_idx, targets)[i % 2]
                nc.vector.tensor_copy(dst[:, b * 128:(b + 1) * 128], ps_y[i % 2][:, 0:128]).then_inc(prep_ev, 1)
            dve.wait_ge(ends_loaded, 16)
            firsts = ends_bc[:, 0, :].rearrange("p (c j) -> p c j", j=TILES)[:, :, 0]
            once(nc.vector.tensor_scalar(ends_cmp[:, :], firsts, thresholds[:, :], None, ALU.is_lt))
            once(nc.vector.tensor_reduce(bounds_f[:, 0:1], ends_cmp[:, :], axis=AX.X, op=ALU.add))
            dve.wait_ge(bounds_tr, 1)
            row = bounds_row
            once(nc.vector.tensor_copy(row[:, 0, 0:NW + 1], ps_a[0:1, 0:NW + 1]))
            unsorted = row[:, 1, 0:1]
            is_sorted = row[:, 1, 1:2]
            once(nc.vector.tensor_scalar(unsorted, row[:, 0, NW:NW + 1], 0.5, None, ALU.is_gt))
            once(nc.vector.tensor_scalar(is_sorted, unsorted, -1.0, 1.0, ALU.mult, ALU.add))
            once(nc.vector.tensor_scalar(row[:, 0, 0:NW], row[:, 0, 0:NW], -1.0, 0.0, ALU.add, ALU.max))
            once(nc.vector.memset(row[:, 0, NW - 1:NW], float(CHUNKS - 1)))
            once(nc.vector.memset(row[:, 0, NW:NW + 2], 1.0))
            once(nc.vector.tensor_scalar(row[:, 2, 0:NW], win_base[0:1, :], float(WIN),
                                          float((CHUNKS - 1) / WIN), ALU.add, ALU.mult))
            once(nc.vector.memset(row[:, 2, NW:NW + 2], float(NW)))
            once(nc.vector.tensor_scalar(row[:, 3, 0:NW + 2], row[:, 0, 0:NW + 2], is_sorted, None, ALU.mult))
            once(nc.vector.scalar_tensor_tensor(out=row[:, 4, 0:NW + 2], in0=row[:, 2, 0:NW + 2], scalar=unsorted,
                                                 in1=row[:, 3, 0:NW + 2], op0=ALU.mult, op1=ALU.add))
            nc.vector.tensor_copy(bounds[0:1, 0:NW + 2], row[:, 4, 0:NW + 2]).then_inc(bounds_done, 1)

            dve.wait_ge(gnn_bias_loaded, 16 * 3)
            def phase0(w, parity, half):
                done = dve.snap(w * S_CHAIN)
                chain = Chain(dve_chain, dve)
                dve.wait_ge(x_loaded[parity], half * 16 + 16)
                dve.wait_ge(xn_stored[parity], half * 16)
                chain(nc.vector.bn_stats(stats[:, :], x_in[parity][:, :]), done)
                apart(dve)
                chain(nc.vector.bn_aggr(mv[:, :], stats[:, :]), done)
                nc.vector.tensor_scalar(mv[:, 1:2], mv[:, 1:2], EPS, None, ALU.add).then_inc(var_ready, 1)
                dve.wait_ge(rstd_ready, w * 2 + 1)
                nc.vector.tensor_scalar(xn_in[parity][:, :], x_in[parity][:, :], mv[:, 0:1], rstd[:, :],
                                        ALU.subtract, ALU.mult).then_inc(xn_ready, 1)
                dve.wait_ge(xn_ready, w + 1)
                chain(nc.vector.bn_stats(stats[:, :], xn_in[parity][:, :]), done)
                apart(dve)
                chain(nc.vector.bn_aggr(mv[:, :], stats[:, :]), done)
                nc.vector.tensor_scalar(mv[:, 1:2], mv[:, 1:2], EPS, None, ALU.add).then_inc(var_ready, 1)
                dve.wait_ge(rstd_ready, w * 2 + 2)
                nc.vector.tensor_copy(ln1_scale[:, bass.ds(w, 1)], rstd[:, :])
                nc.vector.scalar_tensor_tensor(out=ln1_shift[:, bass.ds(w, 1)], in0=mv[:, 0:1], scalar=-1.0,
                                               in1=rstd[:, :], op0=ALU.mult, op1=ALU.mult).then_inc(ln1_ready, 1)
                assert chain.n == S_CHAIN
                evac_y(0, w, parity, half)
            windows(dve, phase0)

            def onehots(l, w, first, last):
                with dve.Fori(first, last + 1) as pos:
                    n = dve.snap(((steps * l if l else 0) + pos + w) * TILES)
                    col = dve.snap((pos % CHUNKS) * TILES)
                    for j in range(TILES):
                        dve.wait_ge(onehot_used, n + (j + 1))
                        nc.vector.scalar_tensor_tensor(
                            out=onehot[j][:, :],
                            in0=targets[:, bass.ds(col + j, 1)].broadcast_to([128, WIN]),
                            scalar=win_base[:, bass.ds(w, 1)],
                            in1=iota_win[:, :], op0=ALU.subtract, op1=ALU.is_equal).then_inc(onehot_ready, 1)

            steps = dve.snap(read_int(dve, NW - 1, LAST_TOP) + NW)

            def windows_with_bounds(l, body):
                first = dve.alloc_register(f"first_dve{l}")
                dve.reg_mov(first, 0)
                with dve.Fori(0, NW // 2) as half:
                    for parity in range(2):
                        w = half * 2 + parity
                        last = read_int(dve, w, LAST_TOP)
                        start = dve.snap(first, min_val=0, max_val=LAST_TOP)
                        onehots(l, w, start, last)
                        dve.reg_mov(first, last)
                        body(w, parity, half)

            def phase1(w, parity, half):
                evac_y(1, w, parity, half)
                dve.wait_ge(v_copied, w + 1)
                nc.vector.tensor_copy(qk_all[:, bass.ds(w * K, K), :],
                                      ps_c[0:WIN, 0:K * BDW].rearrange("p (c d) -> p c d", c=K)[:, :, 0:2 * QK]
                                      ).then_inc(qk_copied, 1)
            nc.vector.memset(v_all[:, :, D:VW], 1.0)
            windows_with_bounds(0, phase1)

            dve.wait_ge(qk_copied, NW)
            dve.wait_ge(v_copied, NW)
            q4 = qk_all[:, :, 0:QK].rearrange("p n (h r) -> p n h r", r=KR)
            qmax_b = qk_max[:, :, :].unsqueeze(3).broadcast_to([WIN, NW * K, 4, KR])
            once(nc.vector.tensor_reduce(qk_max[:, :, :], q4, axis=AX.X, op=ALU.max))
            nc.vector.tensor_tensor(q4, q4, qmax_b, ALU.subtract).then_inc(mid_dve, 1)
            k_by_col = qk_all[:, :, QK:2 * QK].rearrange("p (w c) j -> p c j w", c=K)
            nc.vector.tensor_reduce(kmax_part[:, :].rearrange("p (c j) -> p c j", c=K), k_by_col,
                                    axis=AX.X, op=ALU.max).then_inc(mid_ops, 1)
            dve.wait_ge(mid_pe, 1)
            once(nc.vector.tensor_reduce(kmax[:, :], ps_a[0:HK, 0:WIN], axis=AX.X, op=ALU.max))
            nc.vector.tensor_scalar(kdiag[:, :], ident[0:HK, 0:HK], kmax[:, :], None, ALU.mult).then_inc(mid_ops, 1)
            dve.wait_ge(mid_pe, 2)
            kb = ps_b[0:WIN, 0:HK].rearrange("p (c j) -> p c j", c=K)
            for c in range(K):
                last = nc.vector.tensor_tensor(
                    kexp[:, :, c * QK:(c + 1) * QK],
                    qk_all[:, :, QK:2 * QK].rearrange("p (w c) j -> p w c j", c=K)[:, :, c, :],
                    kb[:, c, :].unsqueeze(1).broadcast_to([WIN, NW, QK]), ALU.subtract)
            last.then_inc(mid_dve, 1)
            dve.wait_ge(mid_act, 1)
            once(nc.vector.tensor_reduce(qk_sum[:, :, :], q4, axis=AX.X, op=ALU.add))
            once(nc.vector.reciprocal(qk_sum[:, :, :], qk_sum[:, :, :]))
            nc.vector.tensor_tensor(q4, q4, qk_sum[:, :, :].unsqueeze(3).broadcast_to([WIN, NW * K, 4, KR]),
                                    ALU.mult).then_inc(mid_dve, 1)
            dve.wait_ge(mid_pe, 3)
            once(nc.vector.reciprocal(kv_recip[:, :], ps_c[0:HK, D:VW]))
            once(nc.vector.tensor_scalar(kv_scaled[:, :], ps_c[0:HK, 0:D], kv_recip[:, :], None, ALU.mult))
            nc.vector.tensor_tensor(kv[:, :], kv_scaled[:, :], head_mask[:, :], ALU.mult).then_inc(mid_ops, 1)
            dve.wait_ge(mid_pe, 4)
            nc.vector.tensor_copy(kvT[:, :, :], ps_a[:, 0:K * HK].rearrange("p (k j) -> p k j", k=K)).then_inc(mid_ops, 1)
            dve.wait_ge(mid_pe, 5)
            nc.vector.tensor_copy(kvWo[:, :], ps_b[0:HK, 0:D]).then_inc(mid_ops, 1)

            def phase2(w, parity, half):
                done = dve.snap(w * P2_CHAIN + NW * S_CHAIN)
                chain = Chain(dve_chain, dve)
                dve.wait_ge(xn_loaded[parity], half * 16 + 16 + 16 * (NW // 2))
                dve.wait_ge(x_loaded[parity], half * 16 + 16 + 16 * (NW // 2))
                chain(nc.vector.tensor_tensor(r0[:, :], xn_in[parity][:, :], mix_bc[:, 0, :], ALU.add), done)
                dve.wait_ge(attn_done, w + 1)
                chain(nc.vector.tensor_tensor(fx[:, :], ps_b[0:WIN, 0:D], r0[:, :], ALU.add), done)
                chain(nc.vector.bn_stats(stats[:, :], fx[:, :]), done)
                apart(dve)
                nc.vector.bn_aggr(mv[:, :], stats[:, :]).then_inc(var_ready, 1)
                chain(nc.vector.tensor_tensor(r0[:, :], fx[:, :], x_in[parity][:, :], ALU.add), done)
                chain(nc.vector.tensor_tensor(r0[:, :], r0[:, :], mix_bc[:, 1, :], ALU.add), done)
                dve.wait_ge(std_ready, w + 1)
                chain(nc.vector.reciprocal(small[:, 2:3], rstd[:, :]), done)
                nc.vector.tensor_scalar(xhat[:, :], fx[:, :], mv[:, 0:1], small[:, 2:3],
                                        ALU.subtract, ALU.mult).then_inc(xhat_ready, 1)
                evac_y(2, w, parity, half)
                dve.wait_ge(res_stored, w * 16)
                dve.wait_ge(ffo_done, w + 1)
                nc.vector.tensor_tensor(res_win[:, :], ps_a[0:WIN, 0:D], r0[:, :], ALU.add).then_inc(res_ready, 1)
                assert chain.n == P2_CHAIN
            windows_with_bounds(1, phase2)

            def phase3(w, parity, half):
                done = dve.snap(w * P3_CHAIN + NW * (S_CHAIN + P2_CHAIN))
                chain = Chain(dve_chain, dve)
                dve.wait_ge(tanh_ready, w + 1)
                chain(nc.vector.tensor_scalar(r0[:, :], h_win[:, :], 0.5, 0.5, ALU.mult, ALU.add), done)
                dve.wait_ge(xn_loaded[parity], half * 16 + 16 + 2 * 16 * (NW // 2))
                chain(nc.vector.tensor_tensor(fx[:, :], r0[:, :], xn_in[parity][:, :], ALU.add), done)
                chain(nc.vector.bn_stats(stats[:, :], fx[:, :]), done)
                apart(dve)
                nc.vector.bn_aggr(mv[:, :], stats[:, :]).then_inc(var_ready, 1)
                dve.wait_ge(std_ready, NW + w + 1)
                chain(nc.vector.reciprocal(small[:, 2:3], rstd[:, :]), done)
                nc.vector.tensor_scalar(xhat[:, :], fx[:, :], mv[:, 0:1], small[:, 2:3],
                                        ALU.subtract, ALU.mult).then_inc(t_ready, 1)
                dve.wait_ge(t_ready, w + 1)
                chain(nc.vector.tensor_tensor(acc[:, :], fx[:, :], xhat[:, :], ALU.add), done)
                dve.wait_ge(logits_done, w + 1)
                nc.vector.tensor_reduce(small[:, 0:1], ps_a[0:WIN, 0:E], axis=AX.X, op=ALU.max,
                                        negate=True).then_inc(lmax_ready, 1)
                dve.wait_ge(rexp_ready, w + 1)
                chain(nc.vector.reciprocal(small[:, 4:5], small[:, 1:2]), done)
                chain(nc.vector.tensor_scalar(probs[:, :], probs[:, :], small[:, 4:5], None, ALU.mult), done)
                apart(dve)
                chain(nc.vector.max(out=top8[:, :], in_=probs[:, :]), done)
                apart(dve)
                chain(nc.vector.max_index(out=top8_idx[:, :], in_max=top8[:, :], in_values=probs[:, :]), done)
                chain(nc.vector.tensor_copy(top_idx[:, :], top8_idx[:, 0:2]), done)
                chain(nc.vector.tensor_scalar(small[:, 5:6], top8[:, 0:1], top8[:, 1:2], 1e-12, ALU.add, ALU.max), done)
                chain(nc.vector.reciprocal(small[:, 6:7], small[:, 5:6]), done)
                chain(nc.vector.tensor_scalar(small[:, 8:10], top8[:, 0:2], small[:, 6:7], None, ALU.mult), done)
                for i in range(2):
                    last = nc.vector.tensor_scalar(pick[:, i, :], iota_e[:, :], top_idx[:, i:i + 1],
                                                   small[:, 8 + i:9 + i], ALU.is_equal, ALU.mult)
                chain(last, done)
                nc.vector.tensor_tensor(combine[:, :], pick[:, 0, :], pick[:, 1, :], ALU.add).then_inc(comb_ready, 1)
                dve.wait_ge(comb_ready, w + 1)
                dve.wait_ge(b2_done, w + 1)
                chain(nc.vector.tensor_tensor(acc[:, :], acc[:, :], ps_y[2][0:WIN, 0:D], ALU.add), done)
                for e in range(E):
                    dve.wait_ge(down_done, w * E + (e + 1))
                    if e == E - 1:
                        dve.wait_ge(out_stored[parity], half * 16)
                    dst = out_win[parity] if e == E - 1 else acc
                    last = nc.vector.scalar_tensor_tensor(out=dst[:, :], in0=(ps_b, ps_c)[e % 2][0:WIN, 0:D],
                                                          scalar=combine[:, e:e + 1], in1=acc[:, :],
                                                          op0=ALU.mult, op1=ALU.add)
                    last.then_inc(acc_done, 1)
                    dve.wait_ge(acc_done, w * E + (e + 1))
                assert chain.n == P3_CHAIN
            windows_with_bounds(2, phase3)

        @block.tensor
        def _(pe):
            pe.sem_inc(slots_free, RING)
            pe.sem_inc(onehot_used, TILES)
            pe.wait_ge(consts_made, 5)
            pe.wait_ge(prep_ready, 1)
            for i in range(2 * TB):
                b = i // 2
                if i >= 2:
                    pe.wait_ge(prep_ev, i - 1)
                src = (prep_f, prep_df)[i % 2]
                nc.tensor.transpose(ps_y[i % 2][:, 0:128], src[:, b * 128:(b + 1) * 128], ident[:, :]).then_inc(prep_tr, 1)
            pe.wait_ge(prep_chain, 5)
            nc.tensor.matmul(ps_a[0:1, 0:NW], bounds_f[:, 0:1], ident[0:NW, 0:NW], start=True, stop=True)
            nc.tensor.matmul(ps_a[0:1, NW:NW + 1], order_cnt[:, 0:1], ones_col[:, :], start=True, stop=True).then_inc(bounds_tr, 1)

            def transform(T, src):
                for k in range(K):
                    last = nc.tensor.transpose(ps_tr[:, k * WIN:(k + 1) * WIN], src[:, k * 128:(k + 1) * 128],
                                               ident[0:WIN, 0:WIN])
                last.then_inc(tr_done, 1)

            def products(T):
                pe.wait_ge(hT_ready, T + 1)
                for b in range(5):
                    if b in (0, 2):
                        pe.wait_ge(y_evac_act, T * 3)
                    if b == 3:
                        pe.wait_ge(y_evac_act, T * 3 + 1)
                    if b == 1:
                        pe.wait_ge(y_evac_dve, T * 2)
                    if b == 4:
                        pe.wait_ge(y_evac_dve, T * 2 + 1)
                    n = 2 * D if b < 4 else D
                    for k in range(K):
                        last = nc.tensor.matmul(ps_y[b % 3 if b < 4 else 1][0:WIN, 0:n], hT[:, k, :],
                                                W[:, k, b * 2 * D:b * 2 * D + n], start=(k == 0), stop=(k == K - 1))
                    last.then_inc(y_done, 1)

            pe.wait_ge(W_loaded, 16 * (K + 1))
            pe.wait_ge(prep_ev, 2 * TB)

            def phase0(w, parity, half):
                pe.wait_ge(xn_ready, w + 1)
                transform(w, xn_in[parity])
                products(w)
            windows(pe, phase0)

            steps = pe.snap(read_int(pe, NW - 1, LAST_TOP) + NW)
            layer_positions = pe.snap(read_int(pe, NW, NW) * CHUNKS)
            extra = pe.snap(read_int(pe, NW + 1, NW))

            def scatter(l, w, parity, half, first, last):
                free = {0: (h_ready, 0), 1: (h_ready, NW), 2: (tanh_ready, 0)}[l]
                if l == 2:
                    pe.wait_ge(h_ready, 2 * NW)
                pe.wait_ge(free[0], w + free[1])

                def chunk(pos, start):
                    pe.wait_ge(chunks_ready, pos + (layer_positions * l + 1) if l else pos + 1)
                    n = pe.snap(((steps * l if l else 0) + pos + w) * TILES)
                    slot = pe.snap((pos % RING) * (TILES * D))
                    for j in range(TILES):
                        pe.wait_ge(onehot_ready, n + (j + 1))
                        nc.tensor.matmul(ps_out[0:WIN, 0:D], onehot[j][:, :], ring[:, bass.ds(slot + j * D, D)],
                                         start=(start and j == 0), stop=False).then_inc(onehot_used, 1)
                    return n
                chunk(first, True)
                with pe.If(last > first):
                    with pe.Fori(first + 1, last + 1) as pos:
                        n = chunk(pos, False)
                        pe.wait_ge(onehot_used, n + TILES)
                        pe.sem_inc(slots_free, 1)
                pe.wait_ge(base_loaded[parity], half * 16 + 16 + l * 16 * (NW // 2))
                nc.tensor.matmul(ps_out[0:WIN, 0:D], ident[0:WIN, 0:WIN], base_in[parity][:, :],
                                 start=False, stop=True).then_inc(out_done, 1)

            def windows_with_bounds(l, before, after):
                first = pe.alloc_register(f"first_pe{l}")
                pe.reg_mov(first, 0)
                with pe.Fori(0, NW // 2) as half:
                    for parity in range(2):
                        w = half * 2 + parity
                        before(w, parity, half)
                        last = read_int(pe, w, LAST_TOP)
                        start = pe.snap(first, min_val=0, max_val=LAST_TOP)
                        scatter(l, w, parity, half, start, last)
                        pe.reg_mov(first, last)
                        after(w, parity, half)
                pe.wait_ge(onehot_used, steps * ((l + 1) * TILES) + TILES)
                apart(pe)
                with pe.Fori(0, extra) as _:
                    pe.sem_inc(slots_free, 1)

            def nothing(w, parity, half):
                pass

            pe.wait_ge(mix_loaded, 16 * N_MIX)

            def phase1(w, parity, half):
                pe.wait_ge(xhat_ready, w + 1)
                for k in range(K):
                    last = nc.tensor.transpose(ps_a[:, k * WIN:(k + 1) * WIN], xhat[:, k * 128:(k + 1) * 128],
                                               ident[0:WIN, 0:WIN])
                last.then_inc(mixT_done, 1)
                pe.wait_ge(h_ready, w + 1)
                transform(NW + w, h_win)
                pe.wait_ge(xhatT_ready, w + 1)
                for m in range(K):
                    for k in range(K):
                        last = nc.tensor.matmul(ps_b[:, m * WIN:(m + 1) * WIN], Wx[:, k, m * 128:(m + 1) * 128],
                                                xhatT[:, k, :], start=(k == 0), stop=(k == K - 1))
                last.then_inc(xm_done, 1)
                pe.wait_ge(W_loaded, 16 * (K + 1) * 2)
                products(NW + w)
                pe.wait_ge(xmT_ready, w + 1)
                pe.wait_ge(qk_copied, w)
                pe.wait_ge(v_copied, w)
                for c in range(K):
                    last = nc.tensor.matmul(ps_c[0:WIN, c * BDW:(c + 1) * BDW], xmT[:, c, :], Wqkv[:, :],
                                            start=True, stop=True)
                last.then_inc(qkv_done, 1)
            windows_with_bounds(0, nothing, phase1)

            pe.wait_ge(mid_ops, 1)
            nc.tensor.transpose(ps_a[0:HK, 0:WIN], kmax_part[:, :], ident[0:WIN, 0:WIN]).then_inc(mid_pe, 1)
            pe.wait_ge(mid_ops, 2)
            nc.tensor.matmul(ps_b[0:WIN, 0:HK], ones_row[:, :], kdiag[:, :], start=True, stop=True).then_inc(mid_pe, 1)
            pe.wait_ge(mid_act, 2)
            for w in range(NW):
                last = nc.tensor.matmul(ps_c[0:HK, 0:VW], kexp[:, w, :], v_all[:, w, :],
                                        start=(w == 0), stop=(w == NW - 1))
            last.then_inc(mid_pe, 1)
            pe.wait_ge(mid_ops, 3)
            for k in range(K):
                last = nc.tensor.transpose(ps_a[:, k * HK:(k + 1) * HK], kv[:, k * 128:(k + 1) * 128],
                                           ident[0:HK, 0:HK])
            last.then_inc(mid_pe, 1)
            pe.wait_ge(mid_ops, 4)
            for k in range(K):
                last = nc.tensor.matmul(ps_b[0:HK, 0:D], kvT[:, k, :], Wo[:, k, :], start=(k == 0), stop=(k == K - 1))
            last.then_inc(mid_pe, 1)
            pe.wait_ge(mid_ops, 5)

            def phase2_before(w, parity, half):
                pe.wait_ge(q_ready, w + 1)
                pe.wait_ge(res_ready, w)
                nc.tensor.transpose(ps_a[0:HK, 0:WIN], q_cur[:, :], ident[0:WIN, 0:WIN]).then_inc(qT_done, 1)

            def phase2(w, parity, half):
                pe.wait_ge(qT_ready, w + 1)
                pe.wait_ge(gelu_done, w * FJ)
                nc.tensor.matmul(ps_b[0:WIN, 0:D], qT[:, :], kvWo[:, :], start=True, stop=True).then_inc(attn_done, 1)
                pe.wait_ge(h_ready, NW + w + 1)
                transform(2 * NW + w, h_win)
                pe.wait_ge(W_loaded, 16 * (K + 1) * 3)
                products(2 * NW + w)
                pe.wait_ge(xhat_ready, NW + w + 1)
                for k in range(K):
                    last = nc.tensor.transpose(ps_a[:, k * WIN:(k + 1) * WIN], xhat[:, k * 128:(k + 1) * 128],
                                               ident[0:WIN, 0:WIN])
                last.then_inc(mixT_done, 1)
                pe.wait_ge(xhatT_ready, NW + w + 1)
                for j in range(FJ):
                    bank = (ps_b, ps_c)[j // 4]
                    for k in range(K):
                        last = nc.tensor.matmul(bank[:, (j % 4) * WIN:(j % 4 + 1) * WIN],
                                                W1[:, k, j * 128:(j + 1) * 128], xhatT[:, k, :],
                                                start=(k == 0), stop=(k == K - 1))
                    if j % 4 == 3:
                        last.then_inc(ff_done, 1)
                for j in range(FJ):
                    pe.wait_ge(gelu_done, w * FJ + (j + 1))
                    last = nc.tensor.matmul(ps_a[0:WIN, 0:D], gT[:, j, :], W2[:, j, :],
                                            start=(j == 0), stop=(j == FJ - 1))
                last.then_inc(ffo_done, 1)
            windows_with_bounds(1, phase2_before, phase2)

            pe.wait_ge(moe_loaded, 16 * 2 * E)
            pe.wait_ge(y_evac_act, 3 * 3 * NW)
            pe.wait_ge(y_evac_dve, 3 * 2 * NW)
            pe.wait_ge(res_ready, NW)

            def phase3(w, parity, half):
                pe.wait_ge(t_ready, w + 1)
                transform(3 * NW + w, xhat)
                pe.wait_ge(hT_ready, 3 * NW + w + 1)
                for k in range(K):
                    last = nc.tensor.matmul(ps_a[0:WIN, 0:E], hT[:, k, :], rwT[:, k, :], start=(k == 0), stop=(k == K - 1))
                last.then_inc(logits_done, 1)

                def up(e):
                    if e >= 2:
                        pe.wait_ge(act_done, w * E + (e - 1))
                    for f in range(K):
                        for k in range(K):
                            last = nc.tensor.matmul(ps_y[e % 2][:, f * WIN:(f + 1) * WIN],
                                                    w1e[:, e, k, f * 128:(f + 1) * 128], hT[:, k, :],
                                                    start=(k == 0), stop=(k == K - 1))
                    last.then_inc(up_done, 1)

                def down(e):
                    pe.wait_ge(act_done, w * E + (e + 1))
                    if e >= 2:
                        pe.wait_ge(acc_done, w * E + (e - 1))
                    for f in range(K):
                        last = nc.tensor.matmul((ps_b, ps_c)[e % 2][0:WIN, 0:D], gT[:, (e % 2) * K + f, :],
                                                w2e[:, e, f, :], start=(f == 0), stop=(f == K - 1))
                    last.then_inc(down_done, 1)
                up(0)
                up(1)
                pe.wait_ge(comb_ready, w + 1)
                pe.wait_ge(rexp_ready, w + 1)
                nc.tensor.transpose(ps_a[0:E, 256:256 + WIN], combine[:, :], ident[0:WIN, 0:WIN]).then_inc(combT_done, 1)
                down(0)
                up(2)
                pe.wait_ge(combT_ready, w + 1)
                nc.tensor.matmul(ps_y[2][0:WIN, 0:D], combT[:, :], b2e[:, :], start=True, stop=True).then_inc(b2_done, 1)
                for e in range(3, E):
                    down(e - 2)
                    up(e)
                down(E - 2)
                down(E - 1)
            windows_with_bounds(2, nothing, phase3)


_OUT = "out_0_dram"


def kernel(**inputs):
    import concourse.bacc as bacc
    from concourse.bass_utils import run_bass_kernel_spmd

    nc = bacc.Bacc("TRN2", target_bir_lowering=False, num_devices=1)
    arrays, t = {}, {}
    for name, value in inputs.items():
        a = np.ascontiguousarray(value)
        arrays[f"in_{name}_dram"] = a
        t[name] = nc.dram_tensor(f"in_{name}_dram", a.shape, mybir.dt.from_np(a.dtype), kind="ExternalInput").ap()
    t["out"] = nc.dram_tensor(_OUT, arrays["in_x_dram"].shape, FP32, kind="ExternalOutput").ap()
    gps_program(nc, t)
    r = run_bass_kernel_spmd(nc, [arrays], core_ids=[0])
    return r.results[0][_OUT]
```

```python
import numpy as np
import concourse.bass as bass
from concourse import mybir
from concourse.alu_op_type import AluOpType as ALU
from contextlib import ExitStack

FP32 = mybir.dt.float32
I32 = mybir.dt.int32
U32 = mybir.dt.uint32
ACT = mybir.ActivationFunctionType
AX = mybir.AxisListType
EPS = 1e-5

WIN = 125
WIN_A = 112
TILE = 128
TILES = 2
RING = 13
UNIT = 2
GROUP_A = 7


def gps_program(nc, t):
    nodes, D = t["x"].shape
    edges = t["src"].shape[0]
    R = t["L0_gnn_weights"].shape[1]
    ROWS = R + 1
    K = D // 128
    NW = nodes // WIN
    assert nodes % WIN == 0 and NW % 2 == 0
    body_edges = TILE * TILES * RING
    BODIES = -(-edges // body_edges)
    CHUNKS = BODIES * RING
    while CHUNKS % UNIT:
        BODIES += 1
        CHUNKS += RING
    UNITS = CHUNKS // UNIT
    NT = CHUNKS * TILES
    TB = -(-NT // 128)
    full_tiles = edges // TILE
    rest = edges - full_tiles * TILE
    full_blocks = full_tiles // 128
    last_rows = full_tiles - full_blocks * 128
    H, DH = 8, 32
    KR = t["L0_mix_Wq"].shape[1]
    HK = H * KR
    FF = t["L0_mix_W1"].shape[1]
    FJ = FF // 128
    E = t["L0_ffn_w1"].shape[0]
    PADDED = 1 << 20
    QK = 4 * KR
    BDW = 2 * QK + 128

    table = [nc.dram_tensor(f"table{l}", [nodes * ROWS, D], FP32).ap() for l in range(3)]
    table_nodes = [a.rearrange("(n r) d -> n (r d)", r=ROWS) for a in table]
    xn_dram = nc.dram_tensor("xn_scratch", [nodes, D], FP32).ap()
    res_dram = nc.dram_tensor("res_scratch", [nodes, D], FP32).ap()
    tile_ends_dram = nc.dram_tensor("tile_ends", [2, TB * 128], FP32).ap()

    with ExitStack() as ctx:
        ctx.enter_context(nc.allow_non_contiguous_dma(reason="a few vectors go to a feature a partition"))

        def sb(name, shape, dt=FP32):
            return ctx.enter_context(nc.sbuf_tensor(name, shape, dt))

        def sem(name):
            return ctx.enter_context(nc.semaphore(name))

        ident = sb("ident", [128, 128])
        iota_win = sb("iota_win", [128, WIN])
        win_base = sb("win_base", [128, NW])
        neg_half = sb("neg_half", [WIN, 1])
        zero_col = sb("zero_col", [128, 1])
        act_warm = sb("act_warm", [128, 1])
        ones_row = sb("ones_row", [HK, WIN])
        head_mask = sb("head_mask", [HK, D])
        iota_e = sb("iota_e", [WIN, E])
        gather_idx = sb("gather_idx", [128, TB * 128], I32)
        targets = sb("targets", [128, TB * 128])
        idx_now = sb("idx_now", [128, RING * TILES], U32)
        ring = sb("ring", [128, RING * TILES * D])
        onehot = [sb(f"onehot{i}", [128, TILES, WIN]) for i in range(UNIT)]
        nodes_now = sb("nodes_now", [128, WIN])
        W = sb("W", [128, K, ROWS * D])
        bias_bc = sb("bias_bc", [WIN, 3, D])
        y_stage = [sb(f"y_stage{i}", [WIN, ROWS * D]) for i in range(2)]
        x_in = [sb(f"x_in{i}", [WIN, D]) for i in range(2)]
        xn_in = [sb(f"xn_in{i}", [WIN, D]) for i in range(2)]
        base_in = [sb(f"base_in{i}", [WIN, D]) for i in range(2)]
        hT = [sb(f"hT{i}", [128, K, WIN]) for i in range(2)]
        h_win = sb("h_win", [WIN, D])
        xhat = sb("xhat", [WIN, D])
        xhatT = sb("xhatT", [128, K, WIN])
        xmT = sb("xmT", [128, K, WIN])
        stats = sb("stats", [WIN, 6])
        mv = sb("mv", [WIN, 2])
        rstd = sb("rstd", [WIN, 1])
        ln1_scale = sb("ln1_scale", [WIN, NW])
        ln1_shift = sb("ln1_shift", [WIN, NW])
        Wx = sb("Wx", [128, K, D])
        Wo = sb("Wo", [128, K, D])
        Wqkv = sb("Wqkv", [128, BDW])
        W1 = sb("W1", [128, K, FF])
        W2 = sb("W2", [128, FJ, D])
        cols = sb("cols", [128, 5, K])
        b1_col = sb("b1_col", [128, FJ])
        mix_bc = sb("mix_bc", [WIN, 2, D])
        qk_all = sb("qk_all", [WIN, NW * K, 2 * QK])
        kexp = sb("kexp", [WIN, NW, HK])
        qk_max = sb("qk_max", [WIN, NW * K, 4])
        qk_sum = qk_max
        VW = D + 1
        big_cols = max(NW * VW, 4 * E * D)
        big = sb("big", [128, big_cols])
        v_all = big[0:WIN, 0:NW * VW].rearrange("p (w d) -> p w d", d=VW)
        w1e = big[:, 0:K * E * D].rearrange("p (e k d) -> p e k d", e=E, k=K)
        w2e = big[:, K * E * D:2 * K * E * D].rearrange("p (e k d) -> p e k d", e=E, k=K)
        b1e = sb("b1e", [128, E, K])
        b2e = sb("b2e", [E, D])
        rwT = sb("rwT", [128, K, E])
        kmax_part = sb("kmax_part", [WIN, HK])
        kmax = sb("kmax", [HK, 1])
        kdiag = sb("kdiag", [HK, HK])
        kv_recip = sb("kv_recip", [HK, 1])
        kv_scaled = sb("kv_scaled", [HK, D])
        kv = sb("kv", [HK, D])
        kvT = sb("kvT", [128, K, HK])
        kvWo = sb("kvWo", [HK, D])
        q_cur = sb("q_cur", [WIN, HK])
        qT = sb("qT", [HK, WIN])
        fx = sb("fx", [WIN, D])
        r0 = [sb(f"r0_{i}", [WIN, D]) for i in range(2)]
        gT = sb("gT", [128, FJ, WIN])
        GB = FJ // K
        res_win = sb("res_win", [WIN, D])
        small = sb("small", [WIN, 16])
        newton = sb("newton", [WIN, 5])
        top8 = sb("top8", [WIN, 8])
        top8_idx = sb("top8_idx", [WIN, 8], U32)
        top_idx = sb("top_idx", [WIN, 2])
        probs = sb("probs", [WIN, E])
        pick = sb("pick", [WIN, 2, E])
        combine = sb("combine", [WIN, E])
        combT = sb("combT", [E, WIN])
        acc = [sb(f"acc{i}", [WIN, D]) for i in range(2)]
        NB_INTS = NW + 3
        bounds = sb("bounds", [1, NB_INTS], I32)
        bounds_f = sb("bounds_f", [NW, 8])
        bounds_row = qk_all[0:1, :, :].rearrange("p a b -> p (a b)")[:, 0:5 * NB_INTS].rearrange("p (i n) -> p i n", i=5)

        PREP = TB * 128
        prep_i = big[:, 0:PREP].bitcast(I32)
        prep_f = big[:, PREP:2 * PREP]
        prep_d = big[:, 2 * PREP:3 * PREP].bitcast(I32)
        prep_df = big[:, 3 * PREP:4 * PREP]
        prep_t = big[:, 4 * PREP:5 * PREP].bitcast(I32)
        assert 5 * PREP <= big_cols
        SP_ = max(n for n in range(1, 129) if edges % n == 0)
        ordC = edges // SP_
        assert 3 * ordC <= RING * TILES * D
        order_a = ring[:, 0:ordC].bitcast(I32)
        order_b = ring[:, ordC:2 * ordC].bitcast(I32)
        order_c = ring[:, 2 * ordC:3 * ordC]
        order_cnt = sb("order_cnt", [128, 1])
        ones_col = sb("ones_col", [128, 1])
        ends_bc = big[0:NW, 5 * PREP:5 * PREP + 2 * NT].rearrange("p (i t) -> p i t", i=2)
        ends_cmp = big[0:NW, 5 * PREP + 2 * NT:5 * PREP + 2 * NT + UNITS]
        assert 5 * PREP + 2 * NT + UNITS <= big_cols
        ends_row = sb("ends_row", [128, 2, TB])
        thresholds = sb("thresholds", [NW, 1])

        def ps(name, shape):
            return ctx.enter_context(nc.psum_tensor(name, shape, FP32))
        ps_out = ps("ps_out", [128, 512])
        ps_tr = ps("ps_tr", [128, 512])
        ps_y = [ps(f"ps_y{i}", [128, 512]) for i in range(3)]
        ps_a = ps("ps_a", [128, 512])
        ps_b = ps("ps_b", [128, 512])
        ps_c = ps("ps_c", [128, 512])

        waits_apart = sem("waits_apart")
        consts_made = sem("consts_made")
        prep_zeroed = sem("prep_zeroed")
        edges_loaded = sem("edges_loaded")
        prep_chain = sem("prep_chain")
        prep_ready = sem("prep_ready")
        prep_tr = sem("prep_tr")
        prep_ev = sem("prep_ev")
        ends_stored = sem("ends_stored")
        ends_loaded = sem("ends_loaded")
        bounds_tr = sem("bounds_tr")
        bounds_done = sem("bounds_done")
        W_loaded = sem("W_loaded")
        gnn_bias_loaded = sem("gnn_bias_loaded")
        mix_loaded = sem("mix_loaded")
        moe_loaded = sem("moe_loaded")
        x_loaded = [sem(f"x_loaded{i}") for i in range(2)]
        xn_loaded = [sem(f"xn_loaded{i}") for i in range(2)]
        base_loaded = [sem(f"base_loaded{i}") for i in range(2)]
        var_ready = sem("var_ready")
        rstd_ready = sem("rstd_ready")
        router_chain = sem("router_chain")
        b2_taken = sem("b2_taken")
        dve_chain = sem("dve_chain")
        xn_ready = sem("xn_ready")
        ln1_ready = sem("ln1_ready")
        xn_stored = [sem(f"xn_stored{i}") for i in range(2)]
        tr_done = sem("tr_done")
        hT_ready = sem("hT_ready")
        y_done = sem("y_done")
        y_evac_act = sem("y_evac_act")
        y_evac_dve = sem("y_evac_dve")
        table_stored = [sem(f"table_stored{i}") for i in range(2)]
        idx_loaded = [sem("idx_loaded_a"), sem("idx_loaded_b")]
        gathered = [sem(f"gathered{s}") for s in range(RING)]
        chunks_ready = sem("chunks_ready")
        slots_free = sem("slots_free")
        onehot_ready = sem("onehot_ready")
        nodes_set = sem("nodes_set")
        onehot_used = sem("onehot_used")
        out_done = sem("out_done")
        h_ready = sem("h_ready")
        xhat_ready = sem("xhat_ready")
        mixT_done = sem("mixT_done")
        xhatT_ready = sem("xhatT_ready")
        xm_done = sem("xm_done")
        xmT_ready = sem("xmT_ready")
        qkv_done = sem("qkv_done")
        qk_copied = sem("qk_copied")
        v_copied = sem("v_copied")
        mid_dve = sem("mid_dve")
        mid_ops = sem("mid_ops")
        mid_act = sem("mid_act")
        mid_pe = sem("mid_pe")
        q_ready = sem("q_ready")
        qT_done = sem("qT_done")
        qT_ready = sem("qT_ready")
        attn_done = sem("attn_done")
        ff_done = sem("ff_done")
        gelu_done = sem("gelu_done")
        ffo_done = sem("ffo_done")
        res_ready = sem("res_ready")
        res_stored = sem("res_stored")
        tanh_ready = sem("tanh_ready")
        t_ready = sem("t_ready")
        logits_done = sem("logits_done")
        lmax_ready = sem("lmax_ready")
        rexp_ready = sem("rexp_ready")
        comb_ready = sem("comb_ready")
        combT_done = sem("combT_done")
        combT_ready = sem("combT_ready")
        b2_done = sem("b2_done")
        up_done = sem("up_done")
        act_done = sem("act_done")
        down_done = sem("down_done")
        acc_done = sem("acc_done")
        out_stored = [sem(f"out_stored{i}") for i in range(2)]

        class Chain:
            def __init__(self, s, eng):
                self.s, self.eng, self.n = s, eng, 0

            def __call__(self, ins, base=0):
                self.n += 1
                ins.then_inc(self.s, 1)
                self.eng.wait_ge(self.s, base + self.n)

        EDGE_DMAS = (3 if full_blocks else 2) * 3 + 3
        N_MIX = 4 + 5 * K + FJ + 2 + 4 * 3 + 2 * E + 1

        def apart(eng):
            eng.sem_inc(waits_apart, 1)

        def stored_before(phase, turn):
            return turn * 32 + phase * 32 * (NW // 2)

        S_CHAIN, P2_CHAIN, P3_CHAIN, R_CHAIN = 4, 15, 13, 9

        block = ctx.enter_context(nc.Block())

        def read_int(eng, at, top):
            ap = bounds[0:1, bass.ds(at, 1)] if not isinstance(at, int) else bounds[0:1, at:at + 1]
            return eng.value_load(ap, min_val=0, max_val=top)

        LAST_TOP = (UNITS - 1) * NW

        def windows(eng, body, tail):
            body((0, 0, 0), None)
            with eng.Fori(0, NW // 2 - 1) as i:
                body((i * 2 + 1, 1, i), (i * 2, 0, i))
                body((i * 2 + 2, 0, i + 1), (i * 2 + 1, 1, i))
            last = (NW - 1, 1, NW // 2 - 1)
            body(last, (NW - 2, 0, NW // 2 - 1))
            tail(last)

        ORDER = (1, 0, 4, 2, 3)
        BANK = (0, 1, 2, 0, 1)

        @block.sync
        def _(sp):
            sp.wait_ge(prep_zeroed, 1)
            for name, dst in (("src", prep_i), ("edge_type_8", prep_t), ("dst", prep_d)):
                a = t[name]
                v = dst[:, 0:TB * 128].rearrange("p (b f) -> p b f", f=128)
                if full_blocks:
                    sp.dma_start(v[:, 0:full_blocks, :], a[0:full_blocks * 128 * TILE]
                                 .rearrange("(b p f) -> p b f", p=128, f=TILE)).then_inc(edges_loaded, 16)
                sp.dma_start(v[0:last_rows, full_blocks, :],
                             a[full_blocks * 128 * TILE:full_tiles * TILE]
                             .rearrange("(p f) -> p f", f=TILE)).then_inc(edges_loaded, 16)
                sp.dma_start(v[last_rows:last_rows + 1, full_blocks, 0:rest],
                             a[full_tiles * TILE:edges].rearrange("(p f) -> p f", p=1)).then_inc(edges_loaded, 16)
            a = t["dst"]
            sp.dma_start(order_a[0:SP_, :], a.rearrange("(p f) -> p f", p=SP_)).then_inc(edges_loaded, 16)
            sp.dma_start(order_b[0:SP_ - 1, :], a[1:1 + (SP_ - 1) * ordC]
                         .rearrange("(p f) -> p f", p=SP_ - 1)).then_inc(edges_loaded, 16)
            sp.dma_start(order_b[SP_ - 1:SP_, 0:ordC - 1], a[1 + (SP_ - 1) * ordC:edges]
                         .rearrange("(p f) -> p f", p=1)).then_inc(edges_loaded, 16)
            sp.wait_ge(ends_stored, 1)
            for i in range(2):
                sp.dma_start(tile_ends_dram[i, :].rearrange("(b p) -> p b", p=128),
                             ends_row[:, i, :]).then_inc(ends_stored, 16)
            sp.wait_ge(ends_stored, 1 + 32)
            sp.dma_start(ends_bc[:, :, :], tile_ends_dram[:, 0:NT].unsqueeze(0)
                         .broadcast_to([NW, 2, NT])).then_inc(ends_loaded, 16)

            sp.wait_ge(prep_ev, 2 * TB)
            groups = ((0, GROUP_A), (GROUP_A, RING))
            for g, (s0, s1) in enumerate(groups):
                sp.dma_start(idx_now[:, s0 * TILES:s1 * TILES],
                             gather_idx[:, s0 * TILES:s1 * TILES].bitcast(U32)).then_inc(idx_loaded[g], 16)
            sp.wait_ge(bounds_done, 1)
            passes = read_int(sp, NW, NW)
            turns = sp.snap(passes * (BODIES * 3))
            with sp.Fori(0, turns) as turn:
                nxt = sp.snap(((turn + 1) % BODIES) * (RING * TILES))
                for g, (s0, s1) in enumerate(groups):
                    for s in range(s0, s1):
                        sp.wait_ge(gathered[s], (turn + 1) * (16 * TILES))
                        sp.sem_inc(chunks_ready, 1)
                    sp.dma_start(idx_now[:, s0 * TILES:s1 * TILES],
                                 gather_idx[:, bass.ds(nxt + s0 * TILES, (s1 - s0) * TILES)]
                                 .bitcast(U32)).then_inc(idx_loaded[g], 16)
            sp.wait_ge(idx_loaded[0], turns * 16 + 16)
            sp.wait_ge(idx_loaded[1], turns * 16 + 16)
            apart(sp)

        @block.gpsimd
        def _(pool):
            lo = full_blocks * 128
            nc.gpsimd.memset(prep_i[:, lo:TB * 128], 0)
            nc.gpsimd.memset(prep_t[:, lo:TB * 128], 0)
            nc.gpsimd.memset(order_b[:, ordC - 1:ordC], PADDED)
            nc.gpsimd.memset(prep_d[:, lo:TB * 128], PADDED).then_inc(prep_zeroed, 1)
            nc.gpsimd.memset(ident[:], 1.0).then_inc(consts_made, 1)
            pool.wait_ge(consts_made, 1)
            nc.gpsimd.affine_select(out=ident[:], in_=ident[:], compare_op=ALU.is_equal, fill=0.0,
                                    base=0, pattern=[[-1, 128]], channel_multiplier=1).then_inc(consts_made, 1)
            nc.gpsimd.iota(iota_win[:, :], pattern=[[1, WIN]], base=0, channel_multiplier=0,
                           allow_small_or_imprecise_dtypes=True)
            nc.gpsimd.iota(win_base[:, :], pattern=[[WIN, NW]], base=0, channel_multiplier=0,
                           allow_small_or_imprecise_dtypes=True)
            nc.gpsimd.iota(iota_e[:, :], pattern=[[1, E]], base=0, channel_multiplier=0,
                           allow_small_or_imprecise_dtypes=True)
            nc.gpsimd.iota(thresholds[:, :], pattern=[[0, 1]], base=WIN, channel_multiplier=WIN,
                           allow_small_or_imprecise_dtypes=True)
            nc.gpsimd.memset(neg_half[:], -0.5)
            nc.gpsimd.memset(zero_col[:], 0.0)
            nc.gpsimd.memset(ones_row[:], 1.0)
            nc.gpsimd.memset(ones_col[:], 1.0)
            nc.gpsimd.memset(Wqkv[:], 0.0)
            nc.gpsimd.memset(head_mask[:], 1.0).then_inc(consts_made, 1)
            pool.wait_ge(consts_made, 3)
            mask = head_mask[:, :].rearrange("p (h d) -> p h d", h=H)
            nc.gpsimd.affine_select(out=mask, in_=mask, compare_op=ALU.is_ge, fill=0.0,
                                    base=0, pattern=[[-KR, H], [0, DH]], channel_multiplier=1).then_inc(consts_made, 1)
            pool.wait_ge(consts_made, 4)
            nc.gpsimd.affine_select(out=mask, in_=mask, compare_op=ALU.is_ge, fill=0.0,
                                    base=KR - 1, pattern=[[KR, H], [0, DH]], channel_multiplier=-1).then_inc(consts_made, 1)
            pool.wait_ge(consts_made, 5)
            with pool.Fori(0, 2 * NW) as i:
                pool.wait_ge(var_ready, i + 1)
                nc.gpsimd.tensor_tensor(rstd[:, :], mv[:, 1:2], neg_half[:, :], ALU.pow).then_inc(rstd_ready, 1)

            pool.wait_ge(bounds_done, 1)
            passes = read_int(pool, NW, NW)
            layer_turns = pool.snap(passes * BODIES)
            for l in range(3):
                for i in range(2):
                    pool.wait_ge(table_stored[i], 32 * (NW // 2) * (l + 1))
                with pool.Fori(0, layer_turns) as i:
                    turn = pool.snap(layer_turns * l + i)
                    for s in range(RING):
                        if s in (0, GROUP_A):
                            pool.wait_ge(idx_loaded[int(s == GROUP_A)], turn * 16 + 16)
                        pool.wait_ge(slots_free, turn * RING + (s + 1))
                        apart(pool)
                        for j in range(TILES):
                            c = s * TILES + j
                            nc.gpsimd.indirect_dma_start(
                                ring[:, c * D:(c + 1) * D], None, table[l],
                                bass.IndirectOffsetOnAxis(ap=idx_now[:, c:c + 1], axis=0)).then_inc(gathered[s], 16)

        @block.scalar
        def _(act):
            def evac_y(phase, win, blocks):
                w, parity, turn = win
                T = w + phase * NW
                if 0 in blocks and not (phase == 0 and isinstance(w, int) and w < 2):
                    act.wait_ge(table_stored[parity], stored_before(phase, turn))
                for b in blocks:
                    act.wait_ge(y_done, T * 5 + (ORDER.index(b) + 1))
                    nc.scalar.copy(y_stage[parity][:, b * 2 * D:(b + 1) * 2 * D],
                                   ps_y[BANK[b]][0:WIN, 0:2 * D]).then_inc(y_evac_act, 1)

            def store_y(phase, win):
                w, parity, _ = win
                T = w + phase * NW
                act.wait_ge(y_evac_act, T * 3 + 3)
                act.wait_ge(y_evac_dve, T * 2 + 2)
                for p0, p1 in ((0, WIN_A), (WIN_A, WIN)):
                    act.dma_start(table_nodes[phase][bass.ds(w * WIN + p0, p1 - p0), :],
                                  y_stage[parity][p0:p1, :]).then_inc(table_stored[parity], 16)

            def warm(function):
                nc.scalar.activation(act_warm[:, :], zero_col[:, :], function)

            def copy_hT(phase, win):
                w, parity, _ = win
                act.wait_ge(tr_done, w + (phase * NW + 1))
                nc.scalar.copy(hT[parity][:, :, :], ps_tr[:, 0:K * WIN].rearrange("p (k n) -> p k n", k=K)
                               ).then_inc(hT_ready, 1)

            def rows(a, w):
                return a[bass.ds(w * WIN, WIN), :]

            def load_W(l):
                for k in range(K):
                    act.dma_start(W[:, k, 0:R * D].rearrange("p (r e) -> p r e", r=R),
                                  t["L0_gnn_weights"][l, :, k * 128:(k + 1) * 128, :]
                                  .rearrange("r p e -> p r e")).then_inc(W_loaded, 16)
                act.dma_start(W[:, :, R * D:ROWS * D],
                              t["L0_gnn_roots"][l].rearrange("(k p) e -> p k e", p=128)).then_inc(W_loaded, 16)

            for i in range(2):
                act.dma_start(x_in[i][:, :], rows(t["x"], i)).then_inc(x_loaded[i], 16)
            load_W(0)
            for l in range(3):
                act.dma_start(bias_bc[:, l, :], t["L0_gnn_biases"][l:l + 1, :].broadcast_to([WIN, D])
                              ).then_inc(gnn_bias_loaded, 16)
            act.wait_ge(consts_made, 5)
            n_mix = 0

            def mix(dst, src):
                nonlocal n_mix
                n_mix += 1
                act.dma_start(dst, src).then_inc(mix_loaded, 16)
            mix(Wx[:, :, :], t["L0_mix_Wx"].rearrange("(k p) e -> p k e", p=128))
            mix(Wo[:, :, :], t["L0_mix_Wo"].rearrange("(k p) e -> p k e", p=128))
            mix(W1[:, :, :], t["L0_mix_W1"].rearrange("(k p) e -> p k e", p=128))
            mix(W2[:, :, :], t["L0_mix_W2"].rearrange("(j p) e -> p j e", p=128))
            for i, name in enumerate(("ln1_g", "ln1_b", "bx", "ln2_g", "ln2_b")):
                for k in range(K):
                    mix(cols[:, i, k:k + 1], t["L0_mix_" + name][k * 128:(k + 1) * 128].unsqueeze(1))
            for j in range(FJ):
                mix(b1_col[:, j:j + 1], t["L0_mix_b1"][j * 128:(j + 1) * 128].unsqueeze(1))
            mix(mix_bc[:, 0, :], t["L0_mix_bo"].unsqueeze(0).broadcast_to([WIN, D]))
            mix(mix_bc[:, 1, :], t["L0_mix_b2"].unsqueeze(0).broadcast_to([WIN, D]))
            for j in range(4):
                mix(Wqkv[j * DH:(j + 1) * DH, j * KR:(j + 1) * KR], t["L0_mix_Wq"])
                mix(Wqkv[j * DH:(j + 1) * DH, QK + j * KR:QK + (j + 1) * KR], t["L0_mix_Wk"])
                mix(Wqkv[j * DH:(j + 1) * DH, 2 * QK + j * DH:2 * QK + (j + 1) * DH], t["L0_mix_Wv"])
            for e in range(E):
                mix(rwT[:, :, e:e + 1], t["L0_ffn_router_w"][e, :].rearrange("(k p) -> p k", p=128).unsqueeze(2))
                mix(b1e[:, e, :].unsqueeze(2), t["L0_ffn_b1"][e, :].rearrange("(k p) -> p k", p=128).unsqueeze(2))
            mix(b2e[:, :], t["L0_ffn_b2"])
            assert n_mix == N_MIX

            def phase0(cur, prev):
                w, parity, turn = cur
                if prev and not (isinstance(w, int) and w == NW - 1):
                    act.wait_ge(xn_ready, w)
                    act.dma_start(x_in[1 - parity][:, :], rows(t["x"], w + 1)).then_inc(x_loaded[1 - parity], 16)
                act.wait_ge(xn_ready, w + 1)
                act.dma_start(rows(xn_dram, w), xn_in[parity][:, :]).then_inc(xn_stored[parity], 16)
                copy_hT(0, cur)
                if prev:
                    phase0_tail(prev)

            def phase0_tail(win):
                evac_y(0, win, (0, 2, 3))
                store_y(0, win)
            windows(act, phase0, phase0_tail)

            act.wait_ge(y_done, 5 * NW)
            load_W(1)
            for i in range(2):
                act.wait_ge(table_stored[i], 32 * (NW // 2))
                act.wait_ge(xn_stored[i], 16 * (NW // 2))
            act.wait_ge(mix_loaded, 16 * n_mix)

            def base_rows(l, w):
                return table_nodes[l][bass.ds(w * WIN, WIN), R * D:ROWS * D]

            def load_base(l, w, parity):
                act.dma_start(base_in[parity][:, :], base_rows(l, w)).then_inc(base_loaded[parity], 16)

            def phase1(cur, prev):
                w, parity, turn = cur
                load_base(0, w, parity)
                if not (isinstance(w, int) and w == NW - 1):
                    if prev:
                        act.wait_ge(xhat_ready, w)
                    act.dma_start(xn_in[1 - parity][:, :], rows(xn_dram, w + 1)).then_inc(xn_loaded[1 - parity], 16)
                act.wait_ge(xn_loaded[parity], turn * 16 + 16)
                nc.scalar.activation(xhat[:, :], xn_in[parity][:, :], ACT.Identity,
                                     scale=ln1_scale[:, bass.ds(w, 1)],
                                     bias=ln1_shift[:, bass.ds(w, 1)]).then_inc(xhat_ready, 1)
                act.wait_ge(mixT_done, w + 1)
                for k in range(K):
                    last = nc.scalar.activation(xhatT[:, k, :], ps_a[:, k * WIN:(k + 1) * WIN], ACT.Identity,
                                                scale=cols[:, 0, k:k + 1], bias=cols[:, 1, k:k + 1])
                last.then_inc(xhatT_ready, 1)
                if prev:
                    evac_y(1, prev, (0,))
                act.wait_ge(xm_done, w + 1)
                for k in range(K):
                    last = nc.scalar.activation(xmT[:, k, :], ps_b[:, k * WIN:(k + 1) * WIN], ACT.Identity,
                                                scale=1.0, bias=cols[:, 2, k:k + 1])
                last.then_inc(xmT_ready, 1)
                act.wait_ge(qkv_done, w + 1)
                nc.scalar.copy(v_all[:, bass.ds(w, 1), 0:D].rearrange("p w (c d) -> p (w c) d", c=K),
                               ps_c[0:WIN, 0:K * BDW].rearrange("p (c d) -> p c d", c=K)[:, :, 2 * QK:BDW]
                               ).then_inc(v_copied, 1)
                if prev:
                    evac_y(1, prev, (2, 3))
                    store_y(1, prev)
                act.wait_ge(out_done, w + 1)
                nc.scalar.activation(h_win[:, :], ps_out[0:WIN, 0:D], ACT.Relu).then_inc(h_ready, 1)
                copy_hT(1, cur)

            def phase1_tail(win):
                evac_y(1, win, (0, 2, 3))
                store_y(1, win)
            act.wait_ge(ln1_ready, NW)
            act.wait_ge(bounds_done, 1)
            act.dma_start(xn_in[0][:, :], rows(xn_dram, 0)).then_inc(xn_loaded[0], 16)
            windows(act, phase1, phase1_tail)

            act.wait_ge(mid_dve, 1)
            nc.scalar.activation(qk_all[:, :, 0:QK], qk_all[:, :, 0:QK], ACT.Exp).then_inc(mid_act, 1)
            act.wait_ge(mid_dve, 2)
            nc.scalar.activation(kexp[:, :, :], kexp[:, :, :], ACT.Exp).then_inc(mid_act, 1)
            act.wait_ge(y_done, 5 * 2 * NW)
            load_W(2)
            for i in range(2):
                act.wait_ge(table_stored[i], 2 * 32 * (NW // 2))
            act.wait_ge(mid_dve, 3)

            XN0 = 16 * (NW // 2)

            def copy_q(w):
                nc.scalar.copy(q_cur[:, :].rearrange("p (c j) -> p c j", c=K),
                               qk_all[:, bass.ds(w * K, K), 0:QK]).then_inc(q_ready, 1)
            copy_q(0)

            def phase2(cur, prev):
                w, parity, turn = cur
                warm(ACT.Gelu)
                load_base(1, w, parity)
                act.dma_start(xn_in[parity][:, :], rows(xn_dram, w)).then_inc(xn_loaded[parity], 16)
                act.dma_start(x_in[parity][:, :], rows(t["x"], w)).then_inc(x_loaded[parity], 16)
                act.wait_ge(qT_done, w + 1)
                nc.scalar.copy(qT[:, :], ps_a[0:HK, 0:WIN]).then_inc(qT_ready, 1)
                if prev:
                    gelus(prev)
                    evac_y(2, prev, (0,))
                act.wait_ge(mixT_done, w + (NW + 1))
                for k in range(K):
                    last = nc.scalar.activation(xhatT[:, k, :], ps_a[:, k * WIN:(k + 1) * WIN], ACT.Identity,
                                                scale=cols[:, 3, k:k + 1], bias=cols[:, 4, k:k + 1])
                last.then_inc(xhatT_ready, 1)
                if prev:
                    evac_y(2, prev, (2, 3))
                    store_y(2, prev)
                    store_res(prev)
                if not (isinstance(w, int) and w == NW - 1):
                    copy_q(w + 1)
                act.wait_ge(out_done, w + (NW + 1))
                nc.scalar.activation(h_win[:, :], ps_out[0:WIN, 0:D], ACT.Relu).then_inc(h_ready, 1)
                copy_hT(2, cur)

            def gelus(win):
                w = win[0]
                for j in range(FJ):
                    if j % 4 == 0:
                        act.wait_ge(ff_done, w * 2 + (j // 4 + 1))
                    bank = (ps_b, ps_c)[j // 4]
                    nc.scalar.activation(gT[:, j, :], bank[:, (j % 4) * WIN:(j % 4 + 1) * WIN], ACT.Gelu,
                                         bias=b1_col[:, j:j + 1]).then_inc(gelu_done, 1)

            def store_res(win):
                w = win[0]
                act.wait_ge(res_ready, w + 1)
                act.dma_start(rows(res_dram, w), res_win[:, :]).then_inc(res_stored, 16)

            def phase2_tail(win):
                evac_y(2, win, (0, 2, 3))
                store_y(2, win)
                gelus(win)
                store_res(win)
            windows(act, phase2, phase2_tail)

            act.wait_ge(mid_pe, 5)
            for e in range(E):
                act.dma_start(w1e[:, e, :, :], t["L0_ffn_w1"][e].rearrange("(k p) f -> p k f", p=128)).then_inc(moe_loaded, 16)
                act.dma_start(w2e[:, e, :, :], t["L0_ffn_w2"][e].rearrange("(k p) f -> p k f", p=128)).then_inc(moe_loaded, 16)
            for i in range(2):
                act.wait_ge(table_stored[i], 3 * 32 * (NW // 2))
            act.wait_ge(res_stored, 16 * NW)

            def phase3(cur, prev):
                w, parity, turn = cur
                load_base(2, w, parity)
                act.dma_start(xn_in[parity][:, :], rows(res_dram, w)).then_inc(xn_loaded[parity], 16)
                if prev:
                    copy_hT(3, prev)
                warm(ACT.Exp)
                act.wait_ge(out_done, w + (2 * NW + 1))
                nc.scalar.activation(h_win[:, :], ps_out[0:WIN, 0:D], ACT.Tanh, scale=0.5).then_inc(tanh_ready, 1)
                if prev:
                    experts(prev)

            def experts(win):
                w, parity, _ = win
                act.wait_ge(lmax_ready, w + 1)
                nc.scalar.activation(probs[:, :], ps_a[0:WIN, 0:E], ACT.Exp, bias=small[:, 0:1],
                                     accum_out=small[:, 1:2]).then_inc(rexp_ready, 1)
                for e in range(E):
                    act.wait_ge(up_done, w * E + (e + 1))
                    if e >= GB:
                        act.wait_ge(down_done, w * E + (e - GB + 1))
                    for f in range(K):
                        last = nc.scalar.activation(gT[:, (e % GB) * K + f, :], ps_y[e % 3][:, f * WIN:(f + 1) * WIN],
                                                    ACT.Gelu, bias=b1e[:, e, f:f + 1])
                    last.then_inc(act_done, 1)
                    if e == 4:
                        act.wait_ge(combT_done, w + 1)
                        nc.scalar.copy(combT[:, :], ps_a[0:E, 256:256 + WIN]).then_inc(combT_ready, 1)
                act.wait_ge(acc_done, w * E + E)
                act.dma_start(rows(t["out"], w), acc[parity][:, :]).then_inc(out_stored[parity], 16)

            def phase3_tail(win):
                copy_hT(3, win)
                experts(win)
            windows(act, phase3, phase3_tail)
            for i in range(2):
                act.wait_ge(out_stored[i], 16 * (NW // 2))

        @block.vector
        def _(dve):
            def evac_y(phase, win):
                w, parity, turn = win
                T = w + phase * NW
                if not (phase == 0 and isinstance(w, int) and w < 2):
                    dve.wait_ge(table_stored[parity], stored_before(phase, turn))
                dve.wait_ge(y_done, T * 5 + 1)
                nc.vector.tensor_copy(y_stage[parity][:, 2 * D:4 * D], ps_y[1][0:WIN, 0:2 * D]).then_inc(y_evac_dve, 1)
                dve.wait_ge(y_done, T * 5 + 3)
                nc.vector.tensor_tensor(y_stage[parity][:, R * D:ROWS * D], ps_y[1][0:WIN, 0:D],
                                        bias_bc[:, phase, :], ALU.add).then_inc(y_evac_dve, 1)

            def rsqrt(chain, done, var):
                v, bits, y, s = (newton[:, i:i + 1] for i in range(4))
                minus_half_v = newton[:, 4:5]
                nc.vector.tensor_scalar(minus_half_v, var, EPS, -0.5, ALU.add, ALU.mult)
                chain(nc.vector.tensor_scalar(v, var, EPS, None, ALU.add), done)
                chain(nc.vector.tensor_scalar(bits.bitcast(I32), v.bitcast(I32), 1, None,
                                              ALU.logical_shift_right), done)
                chain(nc.vector.tensor_scalar(y.bitcast(I32), bits.bitcast(I32), -1.0, float(0x5F3759DF),
                                              ALU.mult, ALU.add), done)
                for _ in range(3):
                    chain(nc.vector.scalar_tensor_tensor(out=s, in0=y, scalar=minus_half_v, in1=y,
                                                         op0=ALU.mult, op1=ALU.mult), done)
                    chain(nc.vector.scalar_tensor_tensor(out=y, in0=s, scalar=1.5, in1=y,
                                                         op0=ALU.add, op1=ALU.mult), done)

            once = Chain(prep_chain, dve)
            dve.wait_ge(edges_loaded, 16 * EDGE_DMAS)
            dve.wait_ge(consts_made, 5)
            nc.vector.scalar_tensor_tensor(out=prep_f, in0=prep_i, scalar=float(ROWS), in1=prep_t,
                                           op0=ALU.mult, op1=ALU.add)
            nc.vector.tensor_copy(prep_df, prep_d).then_inc(prep_ready, 1)
            d3 = prep_d.rearrange("p (b f) -> p b f", f=128)
            nc.vector.tensor_reduce(ends_row[:, 0, :], d3, axis=AX.X, op=ALU.min)
            nc.vector.tensor_reduce(ends_row[:, 1, :], d3, axis=AX.X, op=ALU.max).then_inc(ends_stored, 1)
            once(nc.vector.memset(order_cnt[:], 0.0))
            once(nc.vector.tensor_tensor(order_c[0:SP_, :], order_a[0:SP_, :], order_b[0:SP_, :], ALU.is_gt))
            once(nc.vector.tensor_reduce(order_cnt[0:SP_, :], order_c[0:SP_, :], axis=AX.X, op=ALU.add))
            for i in range(2 * TB):
                b = i // 2
                dve.wait_ge(prep_tr, i + 1)
                dst = (gather_idx, targets)[i % 2]
                nc.vector.tensor_copy(dst[:, b * 128:(b + 1) * 128], ps_y[i % 2][:, 0:128]).then_inc(prep_ev, 1)
            dve.wait_ge(ends_loaded, 16)
            firsts = ends_bc[:, 0, :].rearrange("p (c j) -> p c j", j=TILES * UNIT)[:, :, 0]
            once(nc.vector.tensor_scalar(ends_cmp[:, :], firsts, thresholds[:, :], None, ALU.is_lt))
            once(nc.vector.tensor_reduce(bounds_f[:, 0:1], ends_cmp[:, :], axis=AX.X, op=ALU.add))
            dve.wait_ge(bounds_tr, 1)
            row = bounds_row
            once(nc.vector.tensor_copy(row[:, 0, 0:NW + 1], ps_a[0:1, 0:NW + 1]))
            unsorted = row[:, 1, 0:1]
            is_sorted = row[:, 1, 1:2]
            once(nc.vector.tensor_scalar(unsorted, row[:, 0, NW:NW + 1], 0.5, None, ALU.is_gt))
            once(nc.vector.tensor_scalar(is_sorted, unsorted, -1.0, 1.0, ALU.mult, ALU.add))
            once(nc.vector.tensor_scalar(row[:, 0, 0:NW], row[:, 0, 0:NW], -1.0, 0.0, ALU.add, ALU.max))
            once(nc.vector.memset(row[:, 0, NW - 1:NW], float(UNITS - 1)))
            once(nc.vector.memset(row[:, 0, NW:NW + 2], 1.0))
            once(nc.vector.tensor_scalar(row[:, 2, 0:NW], win_base[0:1, :], float(WIN),
                                          float((UNITS - 1) / WIN), ALU.add, ALU.mult))
            once(nc.vector.memset(row[:, 2, NW:NW + 2], float(NW)))
            once(nc.vector.tensor_scalar(row[:, 3, 0:NW + 2], row[:, 0, 0:NW + 2], is_sorted, None, ALU.mult))
            once(nc.vector.scalar_tensor_tensor(out=row[:, 4, 0:NW + 2], in0=row[:, 2, 0:NW + 2], scalar=unsorted,
                                                 in1=row[:, 3, 0:NW + 2], op0=ALU.mult, op1=ALU.add))
            nc.vector.tensor_copy(bounds[0:1, 0:NW + 2], row[:, 4, 0:NW + 2]).then_inc(bounds_done, 1)

            dve.wait_ge(gnn_bias_loaded, 16 * 3)
            def phase0(cur, prev):
                w, parity, turn = cur
                done = w * S_CHAIN
                chain = Chain(dve_chain, dve)
                dve.wait_ge(x_loaded[parity], turn * 16 + 16)
                if not (isinstance(w, int) and w < 2):
                    dve.wait_ge(xn_stored[parity], turn * 16)
                chain(nc.vector.bn_stats(stats[:, :], x_in[parity][:, :]), done)
                apart(dve)
                chain(nc.vector.bn_aggr(mv[:, :], stats[:, :]), done)
                nc.vector.tensor_scalar(mv[:, 1:2], mv[:, 1:2], EPS, None, ALU.add).then_inc(var_ready, 1)
                dve.wait_ge(rstd_ready, w * 2 + 1)
                nc.vector.tensor_scalar(xn_in[parity][:, :], x_in[parity][:, :], mv[:, 0:1], rstd[:, :],
                                        ALU.subtract, ALU.mult).then_inc(xn_ready, 1)
                dve.wait_ge(xn_ready, w + 1)
                chain(nc.vector.bn_stats(stats[:, :], xn_in[parity][:, :]), done)
                apart(dve)
                chain(nc.vector.bn_aggr(mv[:, :], stats[:, :]), done)
                nc.vector.tensor_scalar(mv[:, 1:2], mv[:, 1:2], EPS, None, ALU.add).then_inc(var_ready, 1)
                dve.wait_ge(rstd_ready, w * 2 + 2)
                nc.vector.tensor_copy(ln1_scale[:, bass.ds(w, 1)], rstd[:, :])
                nc.vector.scalar_tensor_tensor(out=ln1_shift[:, bass.ds(w, 1)], in0=mv[:, 0:1], scalar=-1.0,
                                               in1=rstd[:, :], op0=ALU.mult, op1=ALU.mult).then_inc(ln1_ready, 1)
                assert chain.n == S_CHAIN
                if prev:
                    evac_y(0, prev)
            windows(dve, phase0, lambda win: evac_y(0, win))

            def onehot_unit(l, w, pos):
                n = dve.snap(((steps * l if l else 0) + pos + w) * UNIT)
                col = dve.snap((pos % UNITS) * (TILES * UNIT))
                for u in range(UNIT):
                    dve.wait_ge(onehot_used, n + (u + 1))
                    nc.vector.tensor_tensor(
                        onehot[u][:, :, :],
                        targets[:, bass.ds(col + u * TILES, TILES)].unsqueeze(2).broadcast_to([128, TILES, WIN]),
                        nodes_now[:, :].unsqueeze(1).broadcast_to([128, TILES, WIN]),
                        ALU.is_equal).then_inc(onehot_ready, 1)

            def first_onehots(l, w, first):
                if l or not (isinstance(w, int) and w == 0):
                    dve.wait_ge(onehot_ready, dve.snap(((steps * l if l else 0) + first + w) * UNIT))
                    apart(dve)
                nc.vector.tensor_scalar(nodes_now[:, :], iota_win[:, :], win_base[:, bass.ds(w, 1)], None,
                                        ALU.add).then_inc(nodes_set, 1)
                dve.wait_ge(nodes_set, w + (l * NW + 1))
                apart(dve)
                onehot_unit(l, w, first)

            steps = dve.snap(read_int(dve, NW - 1, LAST_TOP) + NW)

            def phase_windows(l, before, body, tail):
                first = dve.alloc_register(f"first_dve{l}")
                last = dve.alloc_register(f"last_dve{l}")
                dve.reg_mov(first, 0)
                dve.reg_mov(last, read_int(dve, 0, LAST_TOP))
                first_onehots(l, 0, 0)

                def bound(reg):
                    return dve.snap(reg, min_val=0, max_val=LAST_TOP)

                def whole(cur, prev):
                    w = cur[0]
                    before(cur, prev)
                    with dve.Fori(bound(first) + 1, bound(last) + 1) as pos:
                        onehot_unit(l, w, pos)

                    def ahead():
                        if isinstance(w, int) and w == NW - 1:
                            return
                        following = read_int(dve, w + 1, LAST_TOP)
                        dve.reg_mov(first, last)
                        dve.reg_mov(last, following)
                        first_onehots(l, w + 1, bound(first))
                    body(cur, prev, ahead)
                windows(dve, whole, tail)

            def phase1(cur, prev):
                w = cur[0]
                if prev:
                    evac_y(1, prev)
                dve.wait_ge(qkv_done, w + 1)
                dve.wait_ge(v_copied, w + 1)
                nc.vector.tensor_copy(qk_all[:, bass.ds(w * K, K), :],
                                      ps_c[0:WIN, 0:K * BDW].rearrange("p (c d) -> p c d", c=K)[:, :, 0:2 * QK]
                                      ).then_inc(qk_copied, 1)
            nc.vector.memset(v_all[:, :, D:VW], 1.0)
            phase_windows(0, phase1, lambda cur, prev, ahead: ahead(), lambda win: evac_y(1, win))

            dve.wait_ge(qk_copied, NW)
            dve.wait_ge(v_copied, NW)
            q4 = qk_all[:, :, 0:QK].rearrange("p n (h r) -> p n h r", r=KR)
            qmax_b = qk_max[:, :, :].unsqueeze(3).broadcast_to([WIN, NW * K, 4, KR])
            once(nc.vector.tensor_reduce(qk_max[:, :, :], q4, axis=AX.X, op=ALU.max))
            nc.vector.tensor_tensor(q4, q4, qmax_b, ALU.subtract).then_inc(mid_dve, 1)
            k_by_col = qk_all[:, :, QK:2 * QK].rearrange("p (w c) j -> p c j w", c=K)
            nc.vector.tensor_reduce(kmax_part[:, :].rearrange("p (c j) -> p c j", c=K), k_by_col,
                                    axis=AX.X, op=ALU.max).then_inc(mid_ops, 1)
            dve.wait_ge(mid_pe, 1)
            once(nc.vector.tensor_reduce(kmax[:, :], ps_a[0:HK, 0:WIN], axis=AX.X, op=ALU.max))
            nc.vector.tensor_scalar(kdiag[:, :], ident[0:HK, 0:HK], kmax[:, :], None, ALU.mult).then_inc(mid_ops, 1)
            dve.wait_ge(mid_pe, 2)
            kb = ps_b[0:WIN, 0:HK].rearrange("p (c j) -> p c j", c=K)
            for c in range(K):
                last = nc.vector.tensor_tensor(
                    kexp[:, :, c * QK:(c + 1) * QK],
                    qk_all[:, :, QK:2 * QK].rearrange("p (w c) j -> p w c j", c=K)[:, :, c, :],
                    kb[:, c, :].unsqueeze(1).broadcast_to([WIN, NW, QK]), ALU.subtract)
            last.then_inc(mid_dve, 1)
            dve.wait_ge(mid_act, 1)
            once(nc.vector.tensor_reduce(qk_sum[:, :, :], q4, axis=AX.X, op=ALU.add))
            once(nc.vector.reciprocal(qk_sum[:, :, :], qk_sum[:, :, :]))
            nc.vector.tensor_tensor(q4, q4, qk_sum[:, :, :].unsqueeze(3).broadcast_to([WIN, NW * K, 4, KR]),
                                    ALU.mult).then_inc(mid_dve, 1)
            dve.wait_ge(mid_pe, 3)
            once(nc.vector.reciprocal(kv_recip[:, :], ps_c[0:HK, D:VW]))
            once(nc.vector.tensor_scalar(kv_scaled[:, :], ps_c[0:HK, 0:D], kv_recip[:, :], None, ALU.mult))
            nc.vector.tensor_tensor(kv[:, :], kv_scaled[:, :], head_mask[:, :], ALU.mult).then_inc(mid_ops, 1)
            dve.wait_ge(mid_pe, 4)
            nc.vector.tensor_copy(kvT[:, :, :], ps_a[:, 0:K * HK].rearrange("p (k j) -> p k j", k=K)).then_inc(mid_ops, 1)
            dve.wait_ge(mid_pe, 5)
            nc.vector.tensor_copy(kvWo[:, :], ps_b[0:HK, 0:D]).then_inc(mid_ops, 1)

            def phase2(cur, prev):
                w, parity, turn = cur
                done = w * P2_CHAIN + NW * S_CHAIN
                chain = Chain(dve_chain, dve)
                dve.wait_ge(xn_loaded[parity], turn * 16 + (16 + 16 * (NW // 2)))
                dve.wait_ge(x_loaded[parity], turn * 16 + (16 + 16 * (NW // 2)))
                chain(nc.vector.tensor_tensor(fx[:, :], xn_in[parity][:, :], mix_bc[:, 0, :], ALU.add), done)
                dve.wait_ge(attn_done, w + 1)
                chain(nc.vector.tensor_tensor(fx[:, :], ps_a[0:WIN, 0:D], fx[:, :], ALU.add), done)
                chain(nc.vector.bn_stats(stats[:, :], fx[:, :]), done)
                apart(dve)
                chain(nc.vector.bn_aggr(mv[:, :], stats[:, :]), done)
                rsqrt(chain, done, mv[:, 1:2])
                nc.vector.tensor_scalar(xhat[:, :], fx[:, :], mv[:, 0:1], newton[:, 2:3],
                                        ALU.subtract, ALU.mult).then_inc(xhat_ready, 1)
                chain(nc.vector.scalar_tensor_tensor(out=r0[parity][:, :], in0=fx[:, :], scalar=0.5,
                                                     in1=x_in[parity][:, :], op0=ALU.add, op1=ALU.add), done)
                chain(nc.vector.tensor_tensor(r0[parity][:, :], r0[parity][:, :], mix_bc[:, 1, :], ALU.add), done)
                assert chain.n == P2_CHAIN, chain.n
                if prev:
                    residual(prev)
                    evac_y(2, prev)

            def residual(win):
                w, parity, _ = win
                if not (isinstance(w, int) and w == 0):
                    dve.wait_ge(res_stored, w * 16)
                dve.wait_ge(ffo_done, w + 1)
                nc.vector.tensor_tensor(res_win[:, :], ps_tr[0:WIN, 0:D], r0[parity][:, :], ALU.add).then_inc(res_ready, 1)

            def phase2_tail(win):
                evac_y(2, win)
                residual(win)
            phase_windows(1, phase2, lambda cur, prev, ahead: ahead(), phase2_tail)

            def layer_out(cur):
                w, parity, turn = cur
                done = w * P3_CHAIN + NW * (S_CHAIN + P2_CHAIN)
                chain = Chain(dve_chain, dve)
                dve.wait_ge(tanh_ready, w + 1)
                dve.wait_ge(xn_loaded[parity], turn * 16 + (16 + 2 * 16 * (NW // 2)))
                chain(nc.vector.scalar_tensor_tensor(out=fx[:, :], in0=h_win[:, :], scalar=0.5,
                                                     in1=xn_in[parity][:, :], op0=ALU.mult, op1=ALU.add), done)
                chain(nc.vector.bn_stats(stats[:, :], fx[:, :]), done)
                apart(dve)
                chain(nc.vector.bn_aggr(mv[:, :], stats[:, :]), done)
                rsqrt(chain, done, mv[:, 1:2])
                nc.vector.tensor_scalar(xhat[:, :], fx[:, :], mv[:, 0:1], newton[:, 2:3],
                                        ALU.subtract, ALU.mult).then_inc(t_ready, 1)
                dve.wait_ge(t_ready, w + 1)
                if not (isinstance(w, int) and w < 2):
                    dve.wait_ge(out_stored[parity], turn * 16)
                chain(nc.vector.tensor_tensor(acc[parity][:, :], fx[:, :], xhat[:, :], ALU.add), done)
                return chain.n

            def router(win, meanwhile=None):
                w = win[0]
                chain = Chain(router_chain, dve)
                done = w * R_CHAIN
                dve.wait_ge(logits_done, w + 1)
                nc.vector.tensor_reduce(small[:, 0:1], ps_a[0:WIN, 0:E], axis=AX.X, op=ALU.max,
                                        negate=True).then_inc(lmax_ready, 1)
                if meanwhile:
                    meanwhile()
                dve.wait_ge(rexp_ready, w + 1)
                chain(nc.vector.reciprocal(small[:, 4:5], small[:, 1:2]), done)
                chain(nc.vector.tensor_scalar(probs[:, :], probs[:, :], small[:, 4:5], None, ALU.mult), done)
                apart(dve)
                chain(nc.vector.max(out=top8[:, :], in_=probs[:, :]), done)
                apart(dve)
                chain(nc.vector.max_index(out=top8_idx[:, :], in_max=top8[:, :], in_values=probs[:, :]), done)
                chain(nc.vector.tensor_copy(top_idx[:, :], top8_idx[:, 0:2]), done)
                chain(nc.vector.tensor_scalar(small[:, 5:6], top8[:, 0:1], top8[:, 1:2], 1e-12, ALU.add, ALU.max), done)
                chain(nc.vector.reciprocal(small[:, 6:7], small[:, 5:6]), done)
                chain(nc.vector.tensor_scalar(small[:, 8:10], top8[:, 0:2], small[:, 6:7], None, ALU.mult), done)
                for i in range(2):
                    last = nc.vector.tensor_scalar(pick[:, i, :], iota_e[:, :], top_idx[:, i:i + 1],
                                                   small[:, 8 + i:9 + i], ALU.is_equal, ALU.mult)
                chain(last, done)
                nc.vector.tensor_tensor(combine[:, :], pick[:, 0, :], pick[:, 1, :], ALU.add).then_inc(comb_ready, 1)
                dve.wait_ge(comb_ready, w + 1)
                assert chain.n == R_CHAIN, chain.n

            def take(win, experts):
                w, parity, turn = win
                for e in experts:
                    if e % 2 == 0:
                        dve.wait_ge(down_done, w * E + (e + 2))
                    nc.vector.scalar_tensor_tensor(
                        out=acc[parity][:, :], in0=(ps_b, ps_c)[e // 2 % 2][0:WIN, e % 2 * D:(e % 2 + 1) * D],
                        scalar=combine[:, e:e + 1], in1=acc[parity][:, :],
                        op0=ALU.mult, op1=ALU.add).then_inc(acc_done, 1)
                    dve.wait_ge(acc_done, w * E + (e + 1))

            def take_b2(win):
                w, parity, _ = win
                dve.wait_ge(b2_done, w + 1)
                nc.vector.tensor_tensor(acc[parity][:, :], acc[parity][:, :], ps_a[0:WIN, 0:D],
                                        ALU.add).then_inc(b2_taken, 1)
                dve.wait_ge(b2_taken, w + 1)

            def phase3(cur, prev, ahead):
                if prev:
                    router(prev, ahead)
                    take(prev, range(0, 2))
                else:
                    ahead()
                assert layer_out(cur) == P3_CHAIN
                if prev:
                    take(prev, range(2, E // 2))
                    take_b2(prev)
                    take(prev, range(E // 2, E))

            def phase3_tail(win):
                router(win)
                take(win, range(0, E // 2))
                take_b2(win)
                take(win, range(E // 2, E))
            phase_windows(2, lambda cur, prev: None, phase3, phase3_tail)

        @block.tensor
        def _(pe):
            pe.sem_inc(slots_free, RING)
            pe.sem_inc(onehot_used, UNIT)
            pe.wait_ge(consts_made, 5)
            pe.wait_ge(prep_ready, 1)
            for i in range(2 * TB):
                b = i // 2
                if i >= 2:
                    pe.wait_ge(prep_ev, i - 1)
                src = (prep_f, prep_df)[i % 2]
                nc.tensor.transpose(ps_y[i % 2][:, 0:128], src[:, b * 128:(b + 1) * 128], ident[:, :]).then_inc(prep_tr, 1)
            pe.wait_ge(prep_chain, 5)
            nc.tensor.matmul(ps_a[0:1, 0:NW], bounds_f[:, 0:1], ident[0:NW, 0:NW], start=True, stop=True)
            nc.tensor.matmul(ps_a[0:1, NW:NW + 1], order_cnt[:, 0:1], ones_col[:, :], start=True, stop=True).then_inc(bounds_tr, 1)

            def transform(phase, win, src):
                T = win[0] + phase * NW
                if not (isinstance(T, int) and T == 0):
                    pe.wait_ge(hT_ready, T)
                for k in range(K):
                    last = nc.tensor.transpose(ps_tr[:, k * WIN:(k + 1) * WIN], src[:, k * 128:(k + 1) * 128],
                                               ident[0:WIN, 0:WIN])
                last.then_inc(tr_done, 1)

            def products(phase, win, blocks=ORDER):
                w, parity, _ = win
                T = w + phase * NW
                first = isinstance(T, int) and T == 0
                pe.wait_ge(hT_ready, T + 1)
                for b in blocks:
                    if b == 0 and not first:
                        pe.wait_ge(y_evac_act, T * 3)
                    if b == 3:
                        pe.wait_ge(y_evac_act, T * 3 + 1)
                    if b == 1 and not first:
                        pe.wait_ge(y_evac_dve, T * 2)
                    if b == 4:
                        pe.wait_ge(y_evac_dve, T * 2 + 1)
                    n = 2 * D if b < 4 else D
                    for k in range(K):
                        last = nc.tensor.matmul(ps_y[BANK[b]][0:WIN, 0:n], hT[parity][:, k, :],
                                                W[:, k, b * 2 * D:b * 2 * D + n], start=(k == 0), stop=(k == K - 1))
                    last.then_inc(y_done, 1)

            pe.wait_ge(W_loaded, 16 * (K + 1))
            pe.wait_ge(prep_ev, 2 * TB)

            def phase0(cur, prev):
                w, parity, _ = cur
                pe.wait_ge(xn_ready, w + 1)
                transform(0, cur, xn_in[parity])
                if prev:
                    products(0, prev)
            windows(pe, phase0, lambda win: products(0, win))

            steps = pe.snap(read_int(pe, NW - 1, LAST_TOP) + NW)
            layer_positions = pe.snap(read_int(pe, NW, NW) * CHUNKS)
            extra = pe.snap(read_int(pe, NW + 1, NW))

            def scatter(l, cur, first, last):
                w, parity, turn = cur
                free = {0: (h_ready, 0), 1: (h_ready, NW), 2: (tanh_ready, 0)}[l]
                if not (isinstance(w, int) and w == 0):
                    pe.wait_ge(free[0], w + free[1])
                elif l:
                    pe.wait_ge(h_ready, l * NW)

                def unit(pos, start):
                    n = pe.snap(((steps * l if l else 0) + pos + w) * UNIT)
                    for u in range(UNIT):
                        ch = pos * UNIT + u
                        pe.wait_ge(chunks_ready, ch + (layer_positions * l + 1) if l else ch + 1)
                        slot = pe.snap((ch % RING) * (TILES * D))
                        pe.wait_ge(onehot_ready, n + (u + 1))
                        for j in range(TILES):
                            mm = nc.tensor.matmul(ps_out[0:WIN, 0:D], onehot[u][:, j, :],
                                                  ring[:, bass.ds(slot + j * D, D)],
                                                  start=(start and u == 0 and j == 0), stop=False)
                        mm.then_inc(onehot_used, 1)
                    return n
                unit(first, True)
                with pe.If(last > first):
                    with pe.Fori(first + 1, last + 1) as pos:
                        n = unit(pos, False)
                        pe.wait_ge(onehot_used, n + UNIT)
                        pe.sem_inc(slots_free, UNIT)
                pe.wait_ge(base_loaded[parity], turn * 16 + (16 + l * 16 * (NW // 2)))
                nc.tensor.matmul(ps_out[0:WIN, 0:D], ident[0:WIN, 0:WIN], base_in[parity][:, :],
                                 start=False, stop=True).then_inc(out_done, 1)

            def phase_windows(l, before, body, tail):
                first = pe.alloc_register(f"first_pe{l}")
                pe.reg_mov(first, 0)

                def whole(cur, prev):
                    before(cur, prev)
                    last = read_int(pe, cur[0], LAST_TOP)
                    scatter(l, cur, pe.snap(first, min_val=0, max_val=LAST_TOP), last)
                    pe.reg_mov(first, last)
                    body(cur, prev)
                windows(pe, whole, tail)
                pe.wait_ge(onehot_used, steps * ((l + 1) * UNIT) + UNIT)
                apart(pe)
                with pe.Fori(0, extra) as _:
                    pe.sem_inc(slots_free, UNIT)

            pe.wait_ge(mix_loaded, 16 * N_MIX)
            pe.wait_ge(W_loaded, 16 * (K + 1) * 2)

            def phase1(cur, prev):
                w = cur[0]
                pe.wait_ge(xhat_ready, w + 1)
                for k in range(K):
                    last = nc.tensor.transpose(ps_a[:, k * WIN:(k + 1) * WIN], xhat[:, k * 128:(k + 1) * 128],
                                               ident[0:WIN, 0:WIN])
                last.then_inc(mixT_done, 1)
                if prev:
                    products(1, prev, (1, 0))
                pe.wait_ge(xhatT_ready, w + 1)
                for m in range(K):
                    for k in range(K):
                        last = nc.tensor.matmul(ps_b[:, m * WIN:(m + 1) * WIN], Wx[:, k, m * 128:(m + 1) * 128],
                                                xhatT[:, k, :], start=(k == 0), stop=(k == K - 1))
                last.then_inc(xm_done, 1)
                if prev:
                    products(1, prev, (4,))
                pe.wait_ge(xmT_ready, w + 1)
                if prev:
                    pe.wait_ge(qk_copied, w)
                for c in range(K):
                    last = nc.tensor.matmul(ps_c[0:WIN, c * BDW:(c + 1) * BDW], xmT[:, c, :], Wqkv[:, :],
                                            start=True, stop=True)
                last.then_inc(qkv_done, 1)
                if prev:
                    products(1, prev, (2, 3))

            def output_transposed(phase):
                def body(cur, prev):
                    pe.wait_ge(h_ready, cur[0] + ((phase - 1) * NW + 1))
                    transform(phase, cur, h_win)
                return body
            phase_windows(0, phase1, output_transposed(1), lambda win: products(1, win))

            pe.wait_ge(mid_ops, 1)
            nc.tensor.transpose(ps_a[0:HK, 0:WIN], kmax_part[:, :], ident[0:WIN, 0:WIN]).then_inc(mid_pe, 1)
            pe.wait_ge(mid_ops, 2)
            nc.tensor.matmul(ps_b[0:WIN, 0:HK], ones_row[:, :], kdiag[:, :], start=True, stop=True).then_inc(mid_pe, 1)
            pe.wait_ge(mid_act, 2)
            for w in range(NW):
                last = nc.tensor.matmul(ps_c[0:HK, 0:VW], kexp[:, w, :], v_all[:, w, :],
                                        start=(w == 0), stop=(w == NW - 1))
            last.then_inc(mid_pe, 1)
            pe.wait_ge(mid_ops, 3)
            for k in range(K):
                last = nc.tensor.transpose(ps_a[:, k * HK:(k + 1) * HK], kv[:, k * 128:(k + 1) * 128],
                                           ident[0:HK, 0:HK])
            last.then_inc(mid_pe, 1)
            pe.wait_ge(mid_ops, 4)
            for k in range(K):
                last = nc.tensor.matmul(ps_b[0:HK, 0:D], kvT[:, k, :], Wo[:, k, :], start=(k == 0), stop=(k == K - 1))
            last.then_inc(mid_pe, 1)
            pe.wait_ge(mid_ops, 5)

            pe.wait_ge(W_loaded, 16 * (K + 1) * 3)

            def up_projection(win):
                for j in range(FJ):
                    bank = (ps_b, ps_c)[j // 4]
                    for k in range(K):
                        last = nc.tensor.matmul(bank[:, (j % 4) * WIN:(j % 4 + 1) * WIN],
                                                W1[:, k, j * 128:(j + 1) * 128], xhatT[:, k, :],
                                                start=(k == 0), stop=(k == K - 1))
                    if j % 4 == 3:
                        last.then_inc(ff_done, 1)

            def down_projection(win):
                w = win[0]
                pe.wait_ge(hT_ready, w + (2 * NW + 1))
                for j in range(FJ):
                    pe.wait_ge(gelu_done, w * FJ + (j + 1))
                    last = nc.tensor.matmul(ps_tr[0:WIN, 0:D], gT[:, j, :], W2[:, j, :],
                                            start=(j == 0), stop=(j == FJ - 1))
                last.then_inc(ffo_done, 1)

            def phase2(cur, prev):
                w = cur[0]
                pe.wait_ge(q_ready, w + 1)
                nc.tensor.transpose(ps_a[0:HK, 0:WIN], q_cur[:, :], ident[0:WIN, 0:WIN]).then_inc(qT_done, 1)
                if prev:
                    up_projection(prev)
                pe.wait_ge(qT_ready, w + 1)
                nc.tensor.matmul(ps_a[0:WIN, 0:D], qT[:, :], kvWo[:, :], start=True, stop=True).then_inc(attn_done, 1)
                if prev:
                    down_projection(prev)
                    products(2, prev, (1, 0, 4))
                pe.wait_ge(xhat_ready, w + (NW + 1))
                for k in range(K):
                    last = nc.tensor.transpose(ps_a[:, k * WIN:(k + 1) * WIN], xhat[:, k * 128:(k + 1) * 128],
                                               ident[0:WIN, 0:WIN])
                last.then_inc(mixT_done, 1)
                if prev:
                    products(2, prev, (2, 3))
                    pe.wait_ge(res_ready, w)
                pe.wait_ge(xhatT_ready, w + (NW + 1))

            def phase2_tail(win):
                products(2, win)
                up_projection(win)
                down_projection(win)
            phase_windows(1, phase2, output_transposed(2), phase2_tail)

            pe.wait_ge(moe_loaded, 16 * 2 * E)
            pe.wait_ge(y_evac_act, 3 * 3 * NW)
            pe.wait_ge(y_evac_dve, 3 * 2 * NW)
            pe.wait_ge(res_ready, NW)

            def tokens_transposed(win):
                pe.wait_ge(t_ready, win[0] + 1)
                transform(3, win, xhat)

            def experts(win):
                w, parity, _ = win
                pe.wait_ge(hT_ready, w + (3 * NW + 1))
                for k in range(K):
                    last = nc.tensor.matmul(ps_a[0:WIN, 0:E], hT[parity][:, k, :], rwT[:, k, :],
                                            start=(k == 0), stop=(k == K - 1))
                last.then_inc(logits_done, 1)

                def up(e):
                    if e >= 3:
                        pe.wait_ge(act_done, w * E + (e - 2))
                    for f in range(K):
                        for k in range(K):
                            last = nc.tensor.matmul(ps_y[e % 3][:, f * WIN:(f + 1) * WIN],
                                                    w1e[:, e, k, f * 128:(f + 1) * 128], hT[parity][:, k, :],
                                                    start=(k == 0), stop=(k == K - 1))
                    last.then_inc(up_done, 1)

                def down(e):
                    pe.wait_ge(act_done, w * E + (e + 1))
                    if e >= 4 and e % 2 == 0:
                        pe.wait_ge(acc_done, w * E + (e - 2))
                    for f in range(K):
                        last = nc.tensor.matmul((ps_b, ps_c)[e // 2 % 2][0:WIN, e % 2 * D:(e % 2 + 1) * D],
                                                gT[:, (e % GB) * K + f, :],
                                                w2e[:, e, f, :], start=(f == 0), stop=(f == K - 1))
                    last.then_inc(down_done, 1)
                up(0)
                up(1)
                up(2)
                for e in range(3, E + 3):
                    down(e - 3)
                    if e < E:
                        up(e)
                    if e == 5:
                        pe.wait_ge(comb_ready, w + 1)
                        nc.tensor.transpose(ps_a[0:E, 256:256 + WIN], combine[:, :],
                                            ident[0:WIN, 0:WIN]).then_inc(combT_done, 1)
                    if e == 6:
                        pe.wait_ge(combT_ready, w + 1)
                        nc.tensor.matmul(ps_a[0:WIN, 0:D], combT[:, :], b2e[:, :], start=True,
                                         stop=True).then_inc(b2_done, 1)

            def phase3_before(cur, prev):
                if prev:
                    tokens_transposed(prev)

            def phase3_tail(win):
                tokens_transposed(win)
                experts(win)
            phase_windows(2, phase3_before, lambda cur, prev: experts(prev) if prev else None, phase3_tail)



_OUT = "out_0_dram"


def kernel(**inputs):
    import concourse.bacc as bacc
    from concourse.bass_utils import run_bass_kernel_spmd

    nc = bacc.Bacc("TRN2", target_bir_lowering=False, num_devices=1)
    arrays, t = {}, {}
    for name, value in inputs.items():
        a = np.ascontiguousarray(value)
        arrays[f"in_{name}_dram"] = a
        t[name] = nc.dram_tensor(f"in_{name}_dram", a.shape, mybir.dt.from_np(a.dtype), kind="ExternalInput").ap()
    t["out"] = nc.dram_tensor(_OUT, arrays["in_x_dram"].shape, FP32, kind="ExternalOutput").ap()
    gps_program(nc, t)
    r = run_bass_kernel_spmd(nc, [arrays], core_ids=[0])
    return r.results[0][_OUT]
```
